# Optimizing a Trainium2 kernel written in Bass

```python
import numpy as np
import jax
import jax.numpy as jnp

def _softmax(x, axis=-1):
    return jax.nn.softmax(x, axis=axis)

def _gelu(x):
    return jax.nn.gelu(x, approximate=True)

def _silu(x):
    return jax.nn.silu(x)

def _sigmoid(x):
    return jax.nn.sigmoid(x)

def _layernorm(x, axis=-1, eps=1e-05):
    m = jnp.mean(x, axis=axis, keepdims=True)
    v = jnp.var(x, axis=axis, keepdims=True)
    return (x - m) / jnp.sqrt(v + eps)

def _scatter_add(tgt, idx, src, axis=0):
    return tgt.at[idx].add(src)

def _segment_sum(src, seg, n):
    return jax.ops.segment_sum(src, seg, n)
kernel_name = 'mk_gnn_ffn_d1_gnn_r8_3ae52d'

def setup_inputs(seed: int=0):
    np.random.seed(seed)
    _w = jnp.asarray

    def _rec_inputs():
        import jax
        import jax.numpy as jnp
        _gk = jax.random.key(seed)
        x = -0.0002117 + 1 * jax.random.normal(jax.random.fold_in(_gk, 1), (12500, 256), jnp.float32)
        src = jax.random.randint(jax.random.fold_in(_gk, 2), (200000,), 0, 12500, jnp.int32)
        dst = jnp.minimum((12500 * jax.random.uniform(jax.random.fold_in(_gk, 3), (200000,)) ** 2.0).astype(jnp.int32), 99999)
        _o = jnp.argsort(dst, stable=True)
        src = src[_o]
        dst = dst[_o]
        return (x, src, dst)
    x, src, dst = _rec_inputs()

    def _L0_gnn_setup():
        import jax, jax.numpy as jnp
        import numpy as np
        N_NODES = 12500
        key = jax.random.key(seed)
        k1, k2, k3, k4 = jax.random.split(key, 4)
        feat = jax.random.normal(k1, (N_NODES, 256), dtype=jnp.float32)
        bound = float(np.sqrt(6.0 / (256 + 256)))
        weight1 = jax.random.uniform(k2, (256, 256), dtype=jnp.float32, minval=-bound, maxval=bound)
        src = jax.random.randint(k3, (200000,), 0, N_NODES, dtype=jnp.int64)
        dst = jax.random.randint(k4, (200000,), 0, N_NODES, dtype=jnp.int64)
        return {'feat': feat, 'weight1': weight1, 'src': src, 'dst': dst}
    _L0_gnn_all = _L0_gnn_setup()
    _L0_gnn_in = {k: v for k, v in _L0_gnn_all.items() if k in ('weight1',)}
    del _L0_gnn_all

    def _L0_ffn_setup():
        import jax, jax.numpy as jnp
        import numpy as np
        NUM_EXPERTS = 8
        TOP_K = 2
        B, S, D = (8, 1024, 256)

        def _moe(tokens, router_w, w1, b1, w2, b2):
            N = tokens.shape[0]
            E = router_w.shape[0]
            logits = tokens.astype(jnp.float32) @ router_w.astype(jnp.float32).T
            probs = jax.nn.softmax(logits, axis=-1)
            rw, re = jax.lax.top_k(probs, TOP_K)
            if TOP_K > 1:
                rw = rw / jnp.maximum(rw.sum(-1, keepdims=True), 1e-12)
            rw = rw.astype(tokens.dtype)
            combine = jnp.zeros((N, E), tokens.dtype).at[jnp.arange(N)[:, None], re].set(rw)
            out = tokens
            for e in range(E):
                h = jax.nn.gelu(tokens @ w1[e] + b1[e], approximate=False)
                y = h @ w2[e] + b2[e]
                out = out + combine[:, e:e + 1] * y
            return out
        key = jax.random.key(seed)
        ks = jax.random.split(key, 4)
        scale = 1.0 / np.sqrt(D).astype(np.float32)
        return {'input_embeddings': jax.random.normal(ks[0], (B, S, D), jnp.float32), 'router_w': jax.random.normal(ks[1], (NUM_EXPERTS, D), jnp.float32) * scale, 'w1': jax.random.normal(ks[2], (NUM_EXPERTS, D, D), jnp.float32) * scale, 'b1': jnp.zeros((NUM_EXPERTS, D), jnp.float32), 'w2': jax.random.normal(ks[3], (NUM_EXPERTS, D, D), jnp.float32) * scale, 'b2': jnp.zeros((NUM_EXPERTS, D), jnp.float32)}
    _L0_ffn_all = _L0_ffn_setup()
    _L0_ffn_in = {k: v for k, v in _L0_ffn_all.items() if k in ('router_w', 'w1', 'b1', 'w2', 'b2')}
    del _L0_ffn_all
    return {'x': x, 'src': src, 'dst': dst, 'L0_gnn_weight1': _L0_gnn_in['weight1'], 'L0_ffn_router_w': _L0_ffn_in['router_w'], 'L0_ffn_w1': _L0_ffn_in['w1'], 'L0_ffn_b1': _L0_ffn_in['b1'], 'L0_ffn_w2': _L0_ffn_in['w2'], 'L0_ffn_b2': _L0_ffn_in['b2']}

def reference(x, src, dst, L0_gnn_weight1, L0_ffn_router_w, L0_ffn_w1, L0_ffn_b1, L0_ffn_w2, L0_ffn_b2):
    import jax
    import jax.numpy as jnp

    def _L0_gnn_ref(feat, weight1, src, dst):
        import jax, jax.numpy as jnp
        import numpy as np
        N_NODES = 12500
        agg = jax.ops.segment_sum(feat[src], dst, num_segments=N_NODES)
        h = (agg + feat) @ weight1
        h = jax.nn.relu(h)
        return h

    def _L0_ffn_ref(input_embeddings, router_w, w1, b1, w2, b2):
        import jax, jax.numpy as jnp
        import numpy as np
        NUM_EXPERTS = 8
        TOP_K = 2
        B, S, D = (8, 1024, 256)

        def _moe(tokens, router_w, w1, b1, w2, b2):
            N = tokens.shape[0]
            E = router_w.shape[0]
            logits = tokens.astype(jnp.float32) @ router_w.astype(jnp.float32).T
            probs = jax.nn.softmax(logits, axis=-1)
            rw, re = jax.lax.top_k(probs, TOP_K)
            if TOP_K > 1:
                rw = rw / jnp.maximum(rw.sum(-1, keepdims=True), 1e-12)
            rw = rw.astype(tokens.dtype)
            combine = jnp.zeros((N, E), tokens.dtype).at[jnp.arange(N)[:, None], re].set(rw)
            out = tokens
            for e in range(E):
                h = jax.nn.gelu(tokens @ w1[e] + b1[e], approximate=False)
                y = h @ w2[e] + b2[e]
                out = out + combine[:, e:e + 1] * y
            return out
        b, s, d = input_embeddings.shape
        tokens = input_embeddings.reshape(b * s, d)
        return _moe(tokens, router_w, w1, b1, w2, b2).reshape(b, s, d)
    x = x + _L0_gnn_ref(_layernorm(x, axis=-1), L0_gnn_weight1, src, dst)
    x = x + _L0_ffn_ref(_layernorm(x, axis=-1)[None], L0_ffn_router_w, L0_ffn_w1, L0_ffn_b1, L0_ffn_w2, L0_ffn_b2)[0]
    return x

_drawn_inputs = setup_inputs


def setup_inputs(seed=0):
    import zlib

    import numpy as np

    out = dict(_drawn_inputs(seed))
    spreads = {'L0_ffn_b1': (0.0, 0.614), 'L0_ffn_b2': (0.0, 0.416)}
    factors = {}
    for name, (base, spread) in spreads.items():
        noise = np.random.default_rng([zlib.crc32(name.encode()), seed]).standard_normal(out[name].shape)
        drawn = base * np.exp(spread * noise) if base else spread * noise
        out[name] = jnp.asarray(drawn.astype(out[name].dtype))
    for name, factor in factors.items():
        out[name] = (out[name] * factor).astype(out[name].dtype)
    return out
```

```python
import concourse.bass as bass
import concourse.mybir as mybir
from concourse.alu_op_type import AluOpType as ALU

ACT = mybir.ActivationFunctionType
F32, F32R, F16 = mybir.dt.float32, mybir.dt.float32r, mybir.dt.float16
I32, U32 = mybir.dt.int32, mybir.dt.uint32

P = 128
D = 256
HALVES = D // P
NODES, EDGES, EXPERTS = 12500, 200000, 8
TILES = -(-NODES // P)
ROWS = TILES * P
CHUNKS = 4
GROUP = CHUNKS * P
SLOTS = 4
ITERS = -(-EDGES // (GROUP * SLOTS))
GROUPS = ITERS * SLOTS
UNITS = TILES + 1
PARTS = SLOTS
LN_TILES = 7
LN_BATCHES = TILES // LN_TILES
EPS = 1e-5
FSCALE = 1024.0
FAR = 1 << 20
SETUP_STEPS = 18
NEWTON = 3
SQRT_STEPS = 4 + 3 * NEWTON
ROUTE_STEPS, FRONT_STEPS = 9, 3 + SQRT_STEPS


def build(nc, x, src, dst, group_max, gw, router, w1, b1, w2, b2, out):
    table = nc.dram_tensor("feature_table", (ROWS, 2 * D), F16, kind="Internal").ap()
    WCOLS = EXPERTS * HALVES * D

    from contextlib import ExitStack
    with ExitStack() as stack:
        def sbuf(name, cols, dtype=F32, parts=P):
            return stack.enter_context(nc.sbuf_tensor(name, [parts, cols], dtype))

        def psum(name, cols=512):
            return stack.enter_context(nc.psum_tensor(name, [P, cols], F32))

        def sem(name):
            return stack.enter_context(nc.semaphore(name))

        park = sbuf("park", TILES * D)
        w1_hi, w1_lo = sbuf("w1_hi", WCOLS, F32R), sbuf("w1_lo", WCOLS, F32R)
        w2_hi, w2_lo = sbuf("w2_hi", WCOLS, F32R), sbuf("w2_lo", WCOLS, F32R)
        gw_sb = sbuf("gw_sb", HALVES * D)
        router_hi, router_lo = sbuf("router_hi", HALVES * EXPERTS, F32R), sbuf("router_lo", HALVES * EXPERTS, F32R)
        router_raw = sbuf("router_raw", HALVES * EXPERTS)
        b1_sb = sbuf("b1_sb", EXPERTS * HALVES)
        b2_sb = sbuf("b2_sb", D, F32, EXPERTS)
        dst_f = sbuf("dst_f", (GROUPS + 1) * CHUNKS)
        tile_base = sbuf("tile_base", TILES + 2)
        group_max_f, group_max_i = sbuf("group_max_f", 4), sbuf("group_max_i", 4, I32)
        last_group = sbuf("last_group", TILES + 2, I32, 1)
        node_row = sbuf("node_row", P, F16)
        part_col = sbuf("part_col", 1)
        ident, ident16 = sbuf("ident", P), sbuf("ident16", P, F16)
        expert_row = sbuf("expert_row", EXPERTS)
        zero_col = sbuf("zero_col", 1, F16)
        ones_col = sbuf("ones_col", 1)
        idx = sbuf("idx", SLOTS * CHUNKS, I32)
        rows = sbuf("rows", SLOTS * CHUNKS * 2 * D, F16)
        onehot = sbuf("onehot", 2 * CHUNKS * P, F16)
        x1, self_rows = sbuf("x1", D), sbuf("self_rows", 2 * D, F16)
        agg = sbuf("agg", D)
        normed, base = sbuf("normed", D), sbuf("base", D)
        tok_hi, tok_lo = sbuf("tok_hi", D, F32R), sbuf("tok_lo", D, F32R)
        gel = sbuf("gel", 2 * D)
        hid_hi, hid_lo = sbuf("hid_hi", 2 * D, F32R), sbuf("hid_lo", 2 * D, F32R)
        acc, acc_out = sbuf("acc", D), sbuf("acc_out", D)
        stats, mv = sbuf("stats", 6 * LN_TILES), sbuf("mv", 2 * LN_TILES)
        half, bits = sbuf("half", LN_TILES), sbuf("bits", LN_TILES, I32)
        rstd, nmr = sbuf("rstd", LN_TILES), sbuf("nmr", LN_TILES)
        logit = sbuf("logit", EXPERTS)
        top, top_i, top_f = sbuf("top", 8), sbuf("top_i", 8, U32), sbuf("top_f", 2)
        lead, tanh, wgt, scratch = sbuf("lead", 1), sbuf("tanh", 1), sbuf("wgt", 2), sbuf("scratch", 1)
        comb_a, comb_b, comb = sbuf("comb_a", EXPERTS), sbuf("comb_b", EXPERTS), sbuf("comb", EXPERTS)
        comb_t = sbuf("comb_t", P, F32, EXPERTS)
        LN = LN_TILES * D
        ln_x = [park[:, k * LN:(k + 1) * LN] for k in (0, 1)]
        ln_f = [park[:, k * LN:(k + 1) * LN] for k in (2, 3)]
        ln_t = [park[:, k * LN:(k + 1) * LN].bitcast(F16) for k in (4, 5)]
        raw_w1 = park[:, 6 * LN:6 * LN + WCOLS]
        raw_w2 = park[:, 6 * LN + WCOLS:6 * LN + 2 * WCOLS]
        dst_i = park[:, 6 * LN + 2 * WCOLS:6 * LN + 2 * WCOLS + GROUPS * CHUNKS].bitcast(I32)
        at = 6 * LN + 2 * WCOLS + GROUPS * CHUNKS
        reaches = park[:, at:at + 4 * TILES]
        sums = psum("sums", 1024)
        ps_h = [psum("ps_h_even"), psum("ps_h_odd")]
        ps_y = [psum("ps_y_even"), psum("ps_y_odd")]
        ps_t = psum("ps_t")
        ps_g = psum("ps_g")
        PS_LOGIT, PS_COMB = slice(256, 264), slice(264, 392)
        x_in = [sem("ln_x_loaded_even"), sem("ln_x_loaded_odd")]
        t_out = [sem("table_stored_even"), sem("table_stored_odd")]
        stats_ready, feat_ready, hi_ready, lo_ready = (sem(n) for n in (
            "ln_scale_ready", "ln_feature_ready", "ln_hi_ready", "ln_lo_ready"))
        ln_step = sem("ln_vector_step")
        consts, weights_in, iotas = sem("small_inputs_loaded"), sem("expert_weights_loaded"), sem("iotas_ready")
        set_up, counted = sem("vector_setup_step"), sem("group_counts_summed")
        w_hi = sem("weight_hi_ready")
        ready = sem("vector_setup_done")
        vector_passed, pool_passed = sem("vector_wait_passed"), sem("pool_wait_passed")
        idx_in = [sem(f"indices_loaded_{u}") for u in range(SLOTS)]
        row_in = [sem(f"rows_gathered_{u}") for u in range(SLOTS)]
        slot_free = [sem(f"slot_free_{u}") for u in range(SLOTS)]
        onehot_ready, onehot_free, parked = sem("onehot_ready"), sem("onehot_free"), sem("tile_parked")
        x_tile, self_tile, stored = sem("x_tile_loaded"), sem("self_rows_loaded"), sem("tile_stored")
        agg_ready, agg_sum, agg_t = sem("agg_loaded"), sem("agg_transposed_sum"), sem("agg_transposed")
        gnn_done, front, normed_ready, base_ready = (sem(n) for n in (
            "graph_product_done", "front_vector_step", "tokens_normed", "base_ready"))
        tok_t, tok_hi_ready, tok_lo_ready = sem("tokens_transposed"), sem("token_hi_ready"), sem("token_lo_ready")
        logits_done, route = sem("logits_done"), sem("route_vector_step")
        lead_ready, tanh_ready = sem("lead_ready"), sem("tanh_of_lead_ready")
        comb_td, comb_tr, bias_done, bias_added = (sem(n) for n in (
            "combine_transposed", "combine_transpose_copied", "bias_sum_done", "bias_sum_added"))
        h_done, gel_ready, hid_hi_ready, hid_lo_ready = (sem(n) for n in (
            "hidden_done", "gelu_ready", "hidden_hi_ready", "hidden_lo_ready"))
        y_done, y_added = sem("expert_output_done"), sem("expert_output_added")
        block = stack.enter_context(nc.Block())

        def wcol(e, k, f=0):
            return (e * HALVES + k) * D + f * P

        def rows_of(t):
            return bass.ds((TILES - 1 - t) * P, P)

        @block.sync
        def _(sp):
            for buf, ap in ((group_max_i[:, :], group_max), (dst_i, dst),
                            (router_raw[:, :].rearrange("p (k e) -> p k e", k=HALVES),
                             router.rearrange("(k p) e -> p k e", p=P)),
                            (gw_sb[:, :].rearrange("p (k d) -> p k d", k=HALVES),
                             gw.rearrange("(k p) d -> p k d", p=P)),
                            (b1_sb[:, :], b1), (b2_sb[:, :], b2)):
                sp.dma_start(buf, ap).then_inc(consts, 16)
            for u in range(SLOTS):
                sp.dma_start(idx[:, u * CHUNKS:(u + 1) * CHUNKS], src[u]).then_inc(idx_in[u], 16)
            xb = x.rearrange("(b t p) d -> b p t d", p=P, t=LN_TILES)

            def load_x(b, k):
                sp.dma_start(ln_x[k].rearrange("p (t d) -> p t d", d=D), xb[b]).then_inc(x_in[k], 16)

            load_x(0, 0)
            load_x(1, 1)
            with sp.Fori(1, LN_BATCHES // 2) as b:
                for k in (0, 1):
                    sp.wait_ge(feat_ready, (2 * b + k - 1) * LN_TILES)
                    load_x(2 * b + k, k)
            for raw, w in ((raw_w1, w1), (raw_w2, w2)):
                sp.dma_start(raw.rearrange("p (k f) -> p k f", f=D),
                             w.rearrange("e (k p) f -> p (e k) f", p=P)).then_inc(weights_in, 16)
            with sp.Fori(0, ITERS - 1) as it:
                for u in range(SLOTS):
                    sp.wait_ge(row_in[u], (it + 1) * (16 * CHUNKS))
                    sp.dma_start(idx[:, u * CHUNKS:(u + 1) * CHUNKS],
                                 src[(it + 1) * SLOTS + u]).then_inc(idx_in[u], 16)

        @block.gpsimd
        def _(pool):
            pool.iota(node_row[:, :], [[1, P]], base=0, channel_multiplier=0,
                      allow_small_or_imprecise_dtypes=True).then_inc(iotas, 1)
            pool.iota(part_col[:, :], [[0, 1]], base=0, channel_multiplier=1,
                      allow_small_or_imprecise_dtypes=True).then_inc(iotas, 1)
            pool.iota(tile_base[:, 0:TILES + 1], [[-P, TILES + 1]], base=(TILES - 1) * P,
                      channel_multiplier=0, allow_small_or_imprecise_dtypes=True).then_inc(iotas, 1)
            pool.iota(expert_row[:, :], [[1, EXPERTS]], base=0, channel_multiplier=0,
                      allow_small_or_imprecise_dtypes=True).then_inc(iotas, 1)

            def lone_wait(sem, value):
                pool.wait_ge(sem, value)
                pool.sem_inc(pool_passed, 1)

            def round_hi(b, k):
                lone_wait(feat_ready, (b + 1) * LN_TILES)
                pool.tensor_copy(ln_t[k].rearrange("p (t c) -> p t c", c=2 * D)[:, :, 0:D],
                                 ln_f[k].rearrange("p (t d) -> p t d", d=D)).then_inc(hi_ready, 1)

            round_hi(0, 0)
            round_hi(1, 1)
            with pool.Fori(1, LN_BATCHES // 2) as b:
                for k in (0, 1):
                    pool.wait_ge(t_out[k], 16 * b)
                    round_hi(2 * b + k, k)
            for k in (0, 1):
                pool.wait_ge(t_out[k], 16 * (LN_BATCHES // 2))

            def gather(it, u):
                lone_wait(idx_in[u], (it + 1) * 16)
                for j in range(CHUNKS):
                    c = u * CHUNKS + j
                    pool.indirect_dma_start(
                        rows[:, c * 2 * D:(c + 1) * 2 * D], None, table,
                        bass.IndirectOffsetOnAxis(ap=idx[:, c:c + 1], axis=0)).then_inc(row_in[u], 16)

            for u in range(SLOTS):
                gather(0, u)
            with pool.Fori(1, ITERS) as it:
                for u in range(SLOTS):
                    pool.wait_ge(slot_free[u], it)
                    gather(it, u)

        @block.vector
        def _(v):
            n = 0

            def own(ins):
                nonlocal n
                n += 1
                ins.then_inc(set_up, 1)

            own(v.memset(last_group[:, :], GROUPS + 1))
            own(v.memset(ones_col[:, :], 1.0))
            own(v.memset(zero_col[:, :], 0.0))
            own(v.memset(dst_f[:, GROUPS * CHUNKS:], float(FAR)))
            own(v.memset(comb[:, :], 0.0))
            own(v.memset(tok_hi[:, :].bitcast(F32), 0.0))
            own(v.memset(tok_lo[:, :].bitcast(F32), 0.0))
            own(v.memset(onehot[:, :], 0.0))
            v.memset(base[:, :], 0.0).then_inc(y_added, 1)
            v.memset(acc_out[:, :], 0.0).then_inc(y_added, 1)
            v.memset(lead[:, :], 0.0).then_inc(base_ready, 1)
            v.memset(scratch[:, :], 0.0).then_inc(parked, 1)
            v.wait_ge(iotas, 4)
            own(v.tensor_scalar(ident[:, :], node_row[:, :], part_col[:, 0:1], None, ALU.is_equal))
            own(v.tensor_scalar(ident16[:, :], node_row[:, :], part_col[:, 0:1], None, ALU.is_equal))
            v.wait_ge(consts, 16 * 6)
            own(v.tensor_copy(group_max_f[:, :], group_max_i[:, :]))
            own(v.tensor_copy(dst_f[:, 0:GROUPS * CHUNKS], dst_i))
            own(v.tensor_copy(router_hi[:, :], router_raw[:, :]))
            v.wait_ge(set_up, n)
            own(v.tensor_tensor(router_lo[:, :], router_raw[:, :], router_hi[:, :].bitcast(F32), ALU.subtract))
            for k in range(4):
                own(v.tensor_scalar(reaches[:, k * TILES:(k + 1) * TILES], tile_base[:, 0:TILES],
                                    group_max_f[:, k:k + 1], None, ALU.is_le))
            assert n == SETUP_STEPS
            v.wait_ge(counted, 1)
            own(v.tensor_scalar(last_group[0:1, 0:TILES], ps_g[0:1, 0:TILES], -1.0, None, ALU.add))

            def lone_wait(sem, value):
                v.wait_ge(sem, value)
                v.sem_inc(vector_passed, 1)

            def inverse_sqrt(y, var, half, bits, sem, first):
                at = first

                def s(ins):
                    nonlocal at
                    at = at + 1
                    ins.then_inc(sem, 1)
                    v.wait_ge(sem, at)
                s(v.tensor_scalar(half, var, EPS, -0.5, ALU.add, ALU.mult))
                s(v.tensor_scalar(y, var, EPS, None, ALU.add))
                s(v.tensor_scalar(bits, y.bitcast(I32), 1, None, ALU.arith_shift_right))
                s(v.tensor_scalar(y.bitcast(I32), bits, -1.0, float(0x5F3759DF), ALU.mult, ALU.add))
                for _ in range(NEWTON):
                    s(v.tensor_tensor(bits.bitcast(F32), y, y, ALU.mult))
                    s(v.tensor_tensor(bits.bitcast(F32), bits.bitcast(F32), half, ALU.mult))
                    s(v.scalar_tensor_tensor(y, bits.bitcast(F32), 1.5, y, ALU.add, ALU.mult))

            def scales(b, k):
                v.wait_ge(x_in[k], (b >> 1) * 16 + 16)
                for t in range(LN_TILES):
                    v.bn_stats(stats[:, 6 * t:6 * t + 6], ln_x[k][:, t * D:(t + 1) * D]).then_inc(ln_step, 1)
                for t in range(LN_TILES):
                    if t == 0:
                        lone_wait(ln_step, b * LN_STEPS + LN_TILES)
                    v.bn_aggr(mv[:, 2 * t:2 * t + 2], stats[:, 6 * t:6 * t + 6]).then_inc(ln_step, 1)
                v.wait_ge(ln_step, b * LN_STEPS + 2 * LN_TILES)
                if not (isinstance(b, int) and b == 0):
                    v.wait_ge(feat_ready, b * LN_TILES)
                inverse_sqrt(rstd[:, :], mv[:, 1:2 * LN_TILES:2], half[:, :], bits[:, :],
                             ln_step, b * LN_STEPS + 2 * LN_TILES)
                v.tensor_scalar(rstd[:, :], rstd[:, :], FSCALE, None, ALU.mult).then_inc(ln_step, 1)
                v.wait_ge(ln_step, (b + 1) * LN_STEPS)
                v.scalar_tensor_tensor(nmr[:, :], mv[:, 0:2 * LN_TILES:2], -1.0, rstd[:, :],
                                       ALU.mult, ALU.mult).then_inc(stats_ready, 1)

            def low(b, k):
                v.wait_ge(hi_ready, b + 1)
                hi_lo = ln_t[k].rearrange("p (t c) -> p t c", c=2 * D)
                v.tensor_tensor(hi_lo[:, :, D:2 * D], ln_f[k].rearrange("p (t d) -> p t d", d=D),
                                hi_lo[:, :, 0:D], ALU.subtract).then_inc(lo_ready, 1)

            LN_STEPS = 2 * LN_TILES + SQRT_STEPS + 1
            scales(0, 0)
            scales(1, 1)
            low(0, 0)
            with v.Fori(1, LN_BATCHES // 2) as b:
                scales(2 * b, 0)
                low(2 * b - 1, 1)
                scales(2 * b + 1, 1)
                low(2 * b, 0)
            low(LN_BATCHES - 1, 1)

            for k, (raw, hi, lo) in enumerate(((raw_w1, w1_hi, w1_lo), (raw_w2, w2_hi, w2_lo))):
                v.wait_ge(w_hi, k + 1)
                own(v.tensor_tensor(lo[:, :], raw, hi[:, :].bitcast(F32), ALU.subtract))
            v.wait_ge(set_up, n)
            v.tensor_copy(scratch[:, :], ones_col[:, :]).then_inc(ready, 1)
            for k in (0, 1):
                v.wait_ge(t_out[k], 16 * (LN_BATCHES // 2))

            step, tile, end, unit, limit = (v.alloc_register(f"v_{r}") for r in (
                "step", "tile", "end", "unit", "limit"))

            def one_hot(group, i):
                s = v.snap(step, min_val=0, max_val=GROUPS + TILES + 2)
                v.wait_ge(onehot_free, s + 1)
                at = (s & 1) * (CHUNKS * P)
                v.scalar_tensor_tensor(
                    onehot[:, bass.ds(at, CHUNKS * P)].rearrange("p (c n) -> p c n", n=P),
                    node_row[:, :].unsqueeze(1).to_broadcast([P, CHUNKS, P]),
                    tile_base[:, bass.ds(i, 1)],
                    dst_f[:, bass.ds(group * CHUNKS, CHUNKS)].unsqueeze(2).to_broadcast([P, CHUNKS, P]),
                    ALU.add, ALU.is_equal).then_inc(onehot_ready, 1)
                v.reg_add(step, step, 1)

            def tile_value():
                return v.snap(tile, min_val=0, max_val=TILES)

            def load_end():
                v.reg_mov(end, v.value_load(last_group[0:1, bass.ds(tile_value(), 1)], min_val=0, max_val=GROUPS + 1))

            def walk(group):
                with v.While(lambda: v.snap(end) == group):
                    i = v.snap(tile, min_val=0, max_val=TILES - 1)
                    one_hot(group, i + 1)
                    s = v.snap(step, min_val=2, max_val=GROUPS + TILES + 2)
                    v.wait_ge(onehot_free, s + 1)
                    at = (i & 1) * 512
                    v.tensor_reduce(park[:, bass.ds(i * D, D)],
                                    sums[:, bass.ds(at, 2 * D)].rearrange("p (h d) -> p d h", h=2),
                                    mybir.AxisListType.X, ALU.add).then_inc(parked, 1)
                    v.reg_add(tile, tile, 1)
                    load_end()

            def routed(ins, m, k, alone=False):
                ins.then_inc(route, 1)
                (lone_wait if alone else v.wait_ge)(route, m * ROUTE_STEPS + k)

            def top_experts(m):
                v.wait_ge(logits_done, m + 1)
                routed(v.tensor_copy(logit[:, :], ps_t[:, PS_LOGIT]), m, 1, alone=True)
                routed(v.max(top[:, :], logit[:, :]), m, 2, alone=True)
                routed(v.max_index(top_i[:, :], top[:, :], logit[:, :]), m, 3)
                routed(v.tensor_copy(top_f[:, :], top_i[:, 0:2]), m, 4)
                v.tensor_tensor(lead[:, :], top[:, 0:1], top[:, 1:2], ALU.subtract).then_inc(lead_ready, 1)

            def combine_weights(m):
                v.wait_ge(tanh_ready, m + 1)
                routed(v.tensor_scalar(wgt[:, 0:1], tanh[:, :], 0.5, 0.5, ALU.mult, ALU.add), m, 5)
                routed(v.tensor_scalar(wgt[:, 1:2], tanh[:, :], -0.5, 0.5, ALU.mult, ALU.add), m, 6)
                routed(v.tensor_scalar(comb_a[:, :], expert_row[:, :], top_f[:, 0:1], wgt[:, 0:1],
                                       ALU.is_equal, ALU.mult), m, 7)
                routed(v.tensor_scalar(comb_b[:, :], expert_row[:, :], top_f[:, 1:2], wgt[:, 1:2],
                                       ALU.is_equal, ALU.mult), m, 8)
                routed(v.tensor_tensor(comb[:, :], comb_a[:, :], comb_b[:, :], ALU.add), m, 9)

            def hid_low(m, e):
                at = slice((e & 1) * D, (e & 1) * D + D)
                v.wait_ge(hid_hi_ready, m * EXPERTS + e + 1)
                v.tensor_tensor(hid_lo[:, at], gel[:, at], hid_hi[:, at].bitcast(F32),
                                ALU.subtract).then_inc(hid_lo_ready, 1)

            def add_output(m, e):
                v.wait_ge(y_done, m * EXPERTS + e + 1)
                v.wait_ge(y_added, m * EXPERTS + e + 2)
                if e == 3:
                    v.wait_ge(bias_added, m + 1)
                if e == EXPERTS - 1:
                    v.wait_ge(stored, m * 16 + 16)
                so_far = base[:, :] if e == 0 else acc[:, :]
                into = acc_out[:, :] if e == EXPERTS - 1 else acc[:, :]
                v.scalar_tensor_tensor(into, ps_y[e & 1][:, 0:D], comb[:, e:e + 1], so_far,
                                       ALU.mult, ALU.add).then_inc(y_added, 1)

            def part(m, u):
                if u == 0:
                    top_experts(m)
                hid_low(m, 2 * u)
                if u == 0:
                    combine_weights(m)
                if u >= 1:
                    add_output(m, 2 * u - 1)
                hid_low(m, 2 * u + 1)
                if u == 1:
                    v.wait_ge(comb_td, m + 1)
                    v.tensor_copy(comb_t[:, :], ps_t[0:EXPERTS, PS_COMB]).then_inc(comb_tr, 1)
                if u == 2:
                    v.wait_ge(gnn_done, m + 2)
                    v.wait_ge(x_tile, m * 16 + 16)
                    v.scalar_tensor_tensor(x1[:, :], ps_g[:, 0:D], 0.0, x1[:, :],
                                           ALU.max, ALU.add).then_inc(front, 1)
                    v.wait_ge(front, m * FRONT_STEPS + 1)
                    v.bn_stats(stats[:, 0:6], x1[:, :]).then_inc(front, 1)
                    lone_wait(front, m * FRONT_STEPS + 2)
                    v.bn_aggr(mv[:, 0:2], stats[:, 0:6]).then_inc(front, 1)
                    v.wait_ge(front, m * FRONT_STEPS + 3)
                    inverse_sqrt(rstd[:, 0:1], mv[:, 1:2], half[:, 0:1], bits[:, 0:1],
                                 front, m * FRONT_STEPS + 3)
                    v.tensor_scalar(normed[:, :], x1[:, :], mv[:, 0:1], rstd[:, 0:1],
                                    ALU.subtract, ALU.mult).then_inc(normed_ready, 1)
                add_output(m, 2 * u)
                if u == 1:
                    v.wait_ge(bias_done, m + 1)
                    v.wait_ge(y_added, m * EXPERTS + 5)
                    v.tensor_tensor(acc[:, :], acc[:, :], ps_g[:, D:2 * D], ALU.add).then_inc(bias_added, 1)
                if u == 2:
                    v.wait_ge(normed_ready, m + 1)
                    v.tensor_tensor(base[:, :], x1[:, :], normed[:, :], ALU.add).then_inc(base_ready, 1)
                if u == PARTS - 1:
                    v.wait_ge(tok_hi_ready, m + 1)
                    v.tensor_tensor(tok_lo[:, :], ps_t[:, 0:D], tok_hi[:, :].bitcast(F32),
                                    ALU.subtract).then_inc(tok_lo_ready, 1)
                    add_output(m, EXPERTS - 1)

            def unit_value():
                return v.snap(unit, min_val=0, max_val=UNITS - 1)

            v.reg_mov(step, 0)
            v.reg_mov(tile, 0)
            v.reg_mov(unit, 0)
            load_end()
            one_hot(0, 0)
            with v.Fori(0, ITERS) as it:
                v.reg_mov(limit, tile)
                for u in range(SLOTS):
                    group = it * SLOTS + u
                    walk(group)
                    one_hot(group + 1, tile_value())
                    with v.If(v.snap(unit) < v.snap(limit)):
                        part(unit_value(), u)
                        if u == PARTS - 1:
                            v.reg_add(unit, unit, 1)
            v.tensor_copy(scratch[:, :], ones_col[:, :]).then_inc(parked, 1)
            with v.Fori(0, UNITS):
                with v.If(v.snap(unit) < UNITS):
                    for u in range(PARTS):
                        part(unit_value(), u)
                    v.reg_add(unit, unit, 1)

        @block.tensor
        def _(pe):
            pe.wait_ge(set_up, SETUP_STEPS)
            for k in range(4):
                mm = pe.matmul(ps_g[0:1, 0:TILES], ones_col[:, :], reaches[:, k * TILES:(k + 1) * TILES],
                               start=(k == 0), stop=(k == 3))
            mm.then_inc(counted, 1)
            pe.wait_ge(ready, 1)
            for done in (logits_done, agg_sum, gnn_done):
                pe.matmul(ps_t[:, PS_LOGIT], onehot[:, 0:P], onehot[:, 0:EXPERTS],
                          start=True, stop=True).then_inc(done, 1)
            for k in (0, 1):
                pe.matmul(sums[:, 512 * k:512 * k + 512], onehot[:, 512 * k:512 * k + P],
                          onehot[:, 512 * k:512 * k + 512],
                          start=True, stop=True).then_inc(onehot_free, 1)

            step, tile, end, unit, limit = (pe.alloc_register(f"pe_{r}") for r in (
                "step", "tile", "end", "unit", "limit"))

            def tile_value():
                return pe.snap(tile, min_val=0, max_val=TILES)

            def load_end():
                pe.reg_mov(end, pe.value_load(last_group[0:1, bass.ds(tile_value(), 1)], min_val=0, max_val=GROUPS + 1))

            def sum_group(u, first):
                s = pe.snap(step, min_val=0, max_val=GROUPS + TILES + 2)
                at = (s & 1) * (CHUNKS * P)
                bank = (tile_value() & 1) * 512
                pe.wait_ge(onehot_ready, s + 1)
                for j in range(CHUNKS):
                    c = u * CHUNKS + j
                    mm = pe.matmul(sums[:, bass.ds(bank, 2 * D)], onehot[:, bass.ds(at + j * P, P)],
                                   rows[:, c * 2 * D:(c + 1) * 2 * D], start=(first and j == 0),
                                   stop=False, skip_group_check=True)
                mm.then_inc(onehot_free, 1)
                pe.reg_add(step, step, 1)

            def walk(it, u):
                pe.wait_ge(row_in[u], (it + 1) * (16 * CHUNKS))
                sum_group(u, False)
                with pe.While(lambda: pe.snap(end) == it * SLOTS + u):
                    pe.wait_ge(parked, tile_value() + 1)
                    pe.reg_add(tile, tile, 1)
                    load_end()
                    sum_group(u, True)
                pe.matmul(sums[0:1, bass.ds((tile_value() & 1) * 512, 2)], zero_col[:, 0:1], ident16[:, 0:2],
                          start=False, stop=False, skip_group_check=True).then_inc(slot_free[u], 1)

            def hidden(m, e):
                if e == 0:
                    pe.wait_ge(logits_done, m + 1)
                for f in range(HALVES):
                    n = 0
                    for w, t in ((w1_hi, tok_hi), (w1_hi, tok_lo), (w1_lo, tok_hi)):
                        for k in range(HALVES):
                            mm = pe.matmul(ps_h[e & 1][:, f * P:(f + 1) * P],
                                           w[:, wcol(e, k, f):wcol(e, k, f) + P], t[:, k * P:(k + 1) * P],
                                           start=(n == 0), stop=(n == 3 * HALVES - 1))
                            n += 1
                mm.then_inc(h_done, 1)

            def output(m, e):
                pe.wait_ge(hid_lo_ready, m * EXPERTS + e + 1)
                pe.wait_ge(y_added, m * EXPERTS + e + 1)
                n = 0
                for h, w in ((hid_hi, w2_hi), (hid_hi, w2_lo), (hid_lo, w2_hi)):
                    for k in range(HALVES):
                        at = (e & 1) * D + k * P
                        mm = pe.matmul(ps_y[e & 1][:, 0:D], h[:, at:at + P], w[:, wcol(e, k):wcol(e, k) + D],
                                       start=(n == 0), stop=(n == 3 * HALVES - 1))
                        n += 1
                mm.then_inc(y_done, 1)

            def transpose_agg(m):
                pe.wait_ge(route, m * ROUTE_STEPS + 1)
                pe.wait_ge(agg_ready, m + 1)
                pe.wait_ge(self_tile, m * 16 + 16)
                for k in range(HALVES):
                    o = ps_t[:, k * P:(k + 1) * P]
                    pe.matmul(o, agg[:, k * P:(k + 1) * P], ident[:, :], start=True, stop=False)
                    pe.matmul(o, self_rows[:, k * P:(k + 1) * P], ident16[:, :], start=False, stop=False)
                    mm = pe.matmul(o, self_rows[:, D + k * P:D + (k + 1) * P], ident16[:, :],
                                   start=False, stop=True)
                mm.then_inc(agg_sum, 1)

            def part(m, u):
                e = 2 * u
                hidden(m, e)
                if u == 0:
                    transpose_agg(m)
                if u >= 1:
                    output(m, e - 1)
                hidden(m, e + 1)
                if u == 1:
                    pe.wait_ge(agg_t, m + 1)
                    for k in range(HALVES):
                        mm = pe.matmul(ps_g[:, 0:D], agg[:, k * P:(k + 1) * P], gw_sb[:, k * D:(k + 1) * D],
                                       start=(k == 0), stop=(k == HALVES - 1))
                    mm.then_inc(gnn_done, 1)
                    pe.wait_ge(route, (m + 1) * ROUTE_STEPS)
                    pe.transpose(ps_t[0:EXPERTS, PS_COMB], comb[:, :], ident[:, :]).then_inc(comb_td, 1)
                if u == PARTS - 1:
                    pe.wait_ge(normed_ready, m + 1)
                    for k in range(HALVES):
                        mm = pe.transpose(ps_t[:, k * P:(k + 1) * P], normed[:, k * P:(k + 1) * P], ident[:, :])
                    mm.then_inc(tok_t, 1)
                output(m, e)
                if u == 1:
                    pe.wait_ge(comb_tr, m + 1)
                    pe.matmul(ps_g[:, D:2 * D], comb_t[:, :], b2_sb[:, :], start=True, stop=True).then_inc(bias_done, 1)
                if u == PARTS - 1:
                    output(m, e + 1)
                    pe.wait_ge(tok_lo_ready, m + 1)
                    n = 0
                    for t, r in ((tok_hi, router_hi), (tok_lo, router_hi), (tok_hi, router_lo)):
                        for k in range(HALVES):
                            mm = pe.matmul(ps_t[:, PS_LOGIT], t[:, k * P:(k + 1) * P],
                                           r[:, k * EXPERTS:(k + 1) * EXPERTS],
                                           start=(n == 0), stop=(n == 3 * HALVES - 1))
                            n += 1
                    mm.then_inc(logits_done, 1)

            def unit_value():
                return pe.snap(unit, min_val=0, max_val=UNITS - 1)

            pe.reg_mov(step, 0)
            pe.reg_mov(tile, 0)
            pe.reg_mov(unit, 0)
            load_end()
            with pe.Fori(0, ITERS) as it:
                pe.reg_mov(limit, tile)
                for u in range(SLOTS):
                    walk(it, u)
                    with pe.If(pe.snap(unit) < pe.snap(limit)):
                        part(unit_value(), u)
                        if u == PARTS - 1:
                            pe.reg_add(unit, unit, 1)
            with pe.Fori(0, UNITS):
                with pe.If(pe.snap(unit) < UNITS):
                    for u in range(PARTS):
                        part(unit_value(), u)
                    pe.reg_add(unit, unit, 1)

        @block.scalar
        def _(act):
            tb = table.rearrange("(b t p) c -> b p t c", p=P, t=LN_TILES)

            def features(b, k):
                act.wait_ge(stats_ready, b + 1)
                if not isinstance(b, int):
                    act.wait_ge(lo_ready, b - 1)
                for t in range(LN_TILES):
                    act.activation(ln_f[k][:, t * D:(t + 1) * D], ln_x[k][:, t * D:(t + 1) * D], ACT.Identity,
                                   bias=nmr[:, t:t + 1], scale=rstd[:, t:t + 1]).then_inc(feat_ready, 1)

            def store(b, k):
                act.wait_ge(lo_ready, b + 1)
                act.dma_start(tb[b], ln_t[k].rearrange("p (t c) -> p t c", c=2 * D)).then_inc(t_out[k], 16)

            features(0, 0)
            features(1, 1)
            with act.Fori(1, LN_BATCHES // 2) as b:
                store(2 * b - 2, 0)
                features(2 * b, 0)
                store(2 * b - 1, 1)
                features(2 * b + 1, 1)
            store(LN_BATCHES - 2, 0)
            store(LN_BATCHES - 1, 1)
            for k, (raw, hi) in enumerate(((raw_w1, w1_hi), (raw_w2, w2_hi))):
                act.wait_ge(weights_in, 32)
                act.activation(hi[:, :], raw, ACT.Copy).then_inc(w_hi, 1)
            for k in (0, 1):
                act.wait_ge(t_out[k], 16 * (LN_BATCHES // 2))
            act.wait_ge(ready, 1)

            def unit(m, t, result):
                act.wait_ge(base_ready, m + 1)
                act.dma_start(x1[:, :], x[rows_of(t)]).then_inc(x_tile, 16)
                act.wait_ge(agg_sum, m + 1)
                act.dma_start(self_rows[:, :], table[rows_of(t)]).then_inc(self_tile, 16)
                act.wait_ge(parked, m + 2)
                act.wait_ge(gnn_done, m + 1)
                act.activation(agg[:, :], park[:, bass.ds(t * D, D)], ACT.Copy).then_inc(agg_ready, 1)
                for e in range(EXPERTS):
                    act.wait_ge(h_done, m * EXPERTS + e + 1)
                    at = (e & 1) * D
                    for f in range(HALVES):
                        g = act.activation(gel[:, at + f * P:at + (f + 1) * P],
                                           ps_h[e & 1][:, f * P:(f + 1) * P], ACT.Gelu,
                                           bias=b1_sb[:, e * HALVES + f:e * HALVES + f + 1])
                    g.then_inc(gel_ready, 1)
                    act.wait_ge(gel_ready, m * EXPERTS + e + 1)
                    act.activation(hid_hi[:, at:at + D], gel[:, at:at + D], ACT.Copy).then_inc(hid_hi_ready, 1)
                    if e == 0:
                        act.wait_ge(lead_ready, m + 1)
                        act.activation(tanh[:, :], lead[:, :], ACT.Tanh, scale=0.5).then_inc(tanh_ready, 1)
                        act.wait_ge(y_added, m * EXPERTS + 2)
                        act.dma_start(out[bass.ds(result * P, P)], acc_out[:, :]).then_inc(stored, 16)
                    if e == 1:
                        act.wait_ge(agg_sum, m + 2)
                        act.activation(agg[:, :], ps_t[:, 0:D], ACT.Copy, scale=1.0 / FSCALE).then_inc(agg_t, 1)
                act.wait_ge(tok_t, m + 1)
                act.activation(tok_hi[:, :], ps_t[:, 0:D], ACT.Copy).then_inc(tok_hi_ready, 1)

            with act.Fori(0, TILES) as i:
                unit(i, i, TILES + 1 - i)
            unit(TILES, TILES - 1, 1)
            act.wait_ge(y_added, UNITS * EXPERTS + 2)
            act.dma_start(out[0:P], acc_out[:, :]).then_inc(stored, 16)
            act.wait_ge(stored, (UNITS + 1) * 16)


def kernel(**inputs):
    import numpy as np
    from concourse import bacc
    from concourse.bass_utils import run_bass_kernel_spmd

    a = {k: np.asarray(v) for k, v in inputs.items()}
    padded = GROUPS * GROUP
    src = np.zeros(padded, np.int32)
    dst = np.full(padded, FAR, np.int32)
    src[padded - EDGES:] = a["src"][::-1]
    dst[padded - EDGES:] = a["dst"][::-1]
    group_max = np.full(4 * P, -1, np.int32)
    group_max[:GROUPS] = dst[::GROUP]
    x = np.zeros((ROWS, D), np.float32)
    x[:NODES] = a["x"]
    arrays = {
        "x": x,
        "src": np.ascontiguousarray(src.reshape(GROUPS, P, CHUNKS)),
        "dst": np.ascontiguousarray(dst.reshape(GROUPS, P, CHUNKS).transpose(1, 0, 2).reshape(P, GROUPS * CHUNKS)),
        "group_max": np.ascontiguousarray(group_max.reshape(4, P).T),
        "gw": a["L0_gnn_weight1"],
        "router": np.ascontiguousarray(a["L0_ffn_router_w"].T),
        "w1": a["L0_ffn_w1"],
        "b1": np.ascontiguousarray(a["L0_ffn_b1"].reshape(EXPERTS, HALVES, P).transpose(2, 0, 1).reshape(P, EXPERTS * HALVES)),
        "w2": a["L0_ffn_w2"],
        "b2": a["L0_ffn_b2"],
    }
    nc = bacc.Bacc("TRN2", target_bir_lowering=False, num_devices=1)
    args = [nc.dram_tensor(f"in_{n}", v.shape, mybir.dt.from_np(v.dtype), kind="ExternalInput").ap()
            for n, v in arrays.items()]
    out = nc.dram_tensor("out_0", (ROWS + 2 * P, D), F32, kind="ExternalOutput").ap()
    build(nc, *args, out)
    r = run_bass_kernel_spmd(nc, [{f"in_{n}": v for n, v in arrays.items()}], core_ids=[0])
    return r.results[0]["out_0"][:NODES]
```

```python
import concourse.bass as bass
import concourse.mybir as mybir
from concourse.alu_op_type import AluOpType as ALU

ACT = mybir.ActivationFunctionType
F32, F32R, F16 = mybir.dt.float32, mybir.dt.float32r, mybir.dt.float16
I32, U32 = mybir.dt.int32, mybir.dt.uint32

P = 128
D = 256
HALVES = D // P
NODES, EDGES, EXPERTS = 12500, 200000, 8
TILES = -(-NODES // P)
ROWS = TILES * P
CHUNKS = 4
GROUP = CHUNKS * P
SLOTS = 8
ITERS = -(-EDGES // (GROUP * SLOTS))
GROUPS = ITERS * SLOTS
RING = 4
PAIRS = TILES // 2
UNITS = PAIRS + 1
D2, P2 = 2 * D, 2 * P
assert SLOTS == EXPERTS
LN_TILES = 7
LN_BATCHES = TILES // LN_TILES
LN_BUFFERS = 3
EPS = 1e-5
FSCALE = 1024.0
FAR = 1 << 20
SETUP_STEPS = 18
NEWTON = 3
SQRT_STEPS, LN_SQRT_STEPS = 3 + 3 * NEWTON, 3 + 4 * NEWTON
ROUTE_STEPS, FRONT_STEPS = 7, 3 + SQRT_STEPS


def build(nc, x, src, dst, group_max, gw, router_t, w1, b1, w2, b2, out):
    table = nc.dram_tensor("feature_table", (ROWS, 2 * D), F16, kind="Internal").ap()
    park = nc.dram_tensor("edge_sums", (ROWS, D), F32, kind="Internal").ap()
    WCOLS = EXPERTS * HALVES * D

    from contextlib import ExitStack
    with ExitStack() as stack:
        def sbuf(name, cols, dtype=F32, parts=P):
            return stack.enter_context(nc.sbuf_tensor(name, [parts, cols], dtype))

        def psum(name, cols=512):
            return stack.enter_context(nc.psum_tensor(name, [P, cols], F32))

        def sem(name):
            return stack.enter_context(nc.semaphore(name))

        w1_hi, w1_lo = sbuf("w1_hi", WCOLS, F32R), sbuf("w1_lo", WCOLS, F32R)
        w2_hi, w2_lo = sbuf("w2_hi", WCOLS, F32R), sbuf("w2_lo", WCOLS, F32R)
        gw_sb = sbuf("gw_sb", HALVES * D)
        router = sbuf("router", 2 * HALVES * EXPERTS, F32R)
        router_raw = sbuf("router_raw", HALVES * EXPERTS)
        b1_sb = sbuf("b1_sb", EXPERTS * HALVES)
        b2_sb = sbuf("b2_sb", D, F32, EXPERTS)
        dst_f = sbuf("dst_f", (GROUPS + 1) * CHUNKS)
        tile_base = sbuf("tile_base", TILES + 2)
        group_max_f, group_max_i = sbuf("group_max_f", 4), sbuf("group_max_i", 4, I32)
        last_group = sbuf("last_group", TILES + 2, I32, 1)
        node_row = sbuf("node_row", P, F16)
        part_col = sbuf("part_col", 1)
        ident, ident16 = sbuf("ident", P), sbuf("ident16", P, F16)
        expert_row = sbuf("expert_row", EXPERTS)
        scratch_act = sbuf("scratch_act", 1)
        zero_col = sbuf("zero_col", 1, F16)
        ones_col = sbuf("ones_col", 1)
        idx = sbuf("idx", SLOTS * CHUNKS, I32)
        onehot = sbuf("onehot", RING * CHUNKS * P, F16)
        x1, self_rows = sbuf("x1", D2), sbuf("self_rows", 2 * D2, F16)
        base = sbuf("base", D2)
        tok_hi, tok_lo = sbuf("tok_hi", D2, F32R), sbuf("tok_lo", D2, F32R)
        hid_hi, hid_lo = sbuf("hid_hi", 2 * D2, F32R), sbuf("hid_lo", 2 * D2, F32R)
        acc, acc_out = sbuf("acc", D2), sbuf("acc_out", D2)
        stats, mv = sbuf("stats", 6 * LN_TILES), sbuf("mv", 4)
        half, work, rstd = sbuf("half", 2), sbuf("work", 2), sbuf("rstd", 2)
        ln_mv, ln_rstd, ln_nmr = (sbuf(n, 2 * LN_BUFFERS * LN_TILES) for n in ("ln_mv", "ln_rstd", "ln_nmr"))
        ln_half, ln_work = sbuf("ln_half", LN_TILES), sbuf("ln_work", LN_TILES)
        logit = sbuf("logit", 2 * EXPERTS)
        top, top_i, top_f = sbuf("top", 16), sbuf("top_i", 16, U32), sbuf("top_f", 4)
        lead, tanh, wgt, scratch = sbuf("lead", 2), sbuf("tanh", 2), sbuf("wgt", 4), sbuf("scratch", 1)
        comb_a, comb_b, comb = (sbuf(n, 2 * EXPERTS) for n in ("comb_a", "comb_b", "comb"))
        comb_t = sbuf("comb_t", P2, F32, EXPERTS)
        LN = LN_TILES * D
        B = LN_BUFFERS
        arena = sbuf("arena", 3 * B * LN + 2 * WCOLS + GROUPS * CHUNKS + 4 * TILES)
        ln_x = [arena[:, k * LN:(k + 1) * LN] for k in range(B)]
        ln_f = [arena[:, k * LN:(k + 1) * LN] for k in range(B, 2 * B)]
        ln_t = [arena[:, k * LN:(k + 1) * LN].bitcast(F16) for k in range(2 * B, 3 * B)]
        at = 3 * B * LN
        raw_w1, raw_w2 = arena[:, at:at + WCOLS], arena[:, at + WCOLS:at + 2 * WCOLS]
        dst_i = arena[:, at + 2 * WCOLS:at + 2 * WCOLS + GROUPS * CHUNKS].bitcast(I32)
        at += 2 * WCOLS + GROUPS * CHUNKS
        reaches = arena[:, at:at + 4 * TILES]
        rows = arena[:, 0:SLOTS * CHUNKS * D].bitcast(F16)
        at = SLOTS * CHUNKS * D
        assert at + 5 * D2 <= 3 * B * LN
        gel = arena[:, at:at + 2 * D2]
        agg = arena[:, at + 2 * D2:at + 3 * D2]
        normed = arena[:, at + 3 * D2:at + 4 * D2]
        staged = arena[:, at + 4 * D2:at + 5 * D2]
        sums = psum("sums", 1024)
        ps_h = [psum("ps_h_even"), psum("ps_h_odd")]
        ps_y = [psum("ps_y_even"), psum("ps_y_odd")]
        ps_t = psum("ps_t")
        ps_g = psum("ps_g")
        x_in = [sem(f"ln_x_loaded_{k}") for k in range(LN_BUFFERS)]
        t_out = [sem(f"table_stored_{k}") for k in range(LN_BUFFERS)]
        stats_ready, feat_ready, hi_ready, lo_ready = (sem(n) for n in (
            "ln_scale_ready", "ln_feature_ready", "ln_hi_ready", "ln_lo_ready"))
        ln_step, moments_ready, ln_scale_step = (sem(n) for n in (
            "ln_vector_step", "ln_moments_ready", "ln_scale_step"))
        consts, weights_in, iotas = sem("small_inputs_loaded"), sem("expert_weights_loaded"), sem("iotas_ready")
        set_up, counted = sem("vector_setup_step"), sem("group_counts_summed")
        w_hi, w_lo = sem("weight_hi_ready"), sem("weight_lo_ready")
        ready = sem("vector_setup_done")
        vector_passed, pool_passed, loads_passed = (sem(n) for n in (
            "vector_wait_passed", "pool_wait_passed", "loads_wait_passed"))
        idx_in = [sem(f"indices_loaded_{u}") for u in range(SLOTS)]
        row_in = [sem(f"rows_gathered_{u}") for u in range(SLOTS)]
        slot_free = [sem(f"slot_free_{u}") for u in range(SLOTS)]
        onehot_ready, onehot_free, parked = sem("onehot_ready"), sem("onehot_free"), sem("tile_parked")
        in_dram = sem("sum_stored")
        x_tile, self_tile, stored = sem("x_tile_loaded"), sem("self_rows_loaded"), sem("tile_stored")
        agg_ready, agg_sum, agg_t = sem("agg_loaded"), sem("agg_transposed_sum"), sem("agg_transposed")
        gnn_done, front, normed_ready, base_ready = (sem(n) for n in (
            "graph_product_done", "front_vector_step", "tokens_normed", "base_ready"))
        tok_t, tok_hi_ready, tok_lo_ready = sem("tokens_transposed"), sem("token_hi_ready"), sem("token_lo_ready")
        logits_done, route = sem("logits_done"), sem("route_vector_step")
        lead_ready, tanh_ready = sem("lead_ready"), sem("tanh_of_lead_ready")
        comb_td, comb_tr, bias_done, bias_added = (sem(n) for n in (
            "combine_transposed", "combine_transpose_copied", "bias_sum_done", "bias_sum_added"))
        h_done, gel_ready, hid_hi_ready, hid_lo_ready = (sem(n) for n in (
            "hidden_done", "gelu_ready", "hidden_hi_ready", "hidden_lo_ready"))
        y_done, y_added = sem("expert_output_done"), sem("expert_output_added")
        block = stack.enter_context(nc.Block())

        def wcol(e, k, f=0):
            return (e * HALVES + k) * D + f * P

        def last_row_pair(pairs):
            return bass.ds(pairs * P2, P2)

        def by_half(ap):
            return ap.rearrange("p (h d) -> p h d", h=2)

        def over_batches(engine, body):
            rounds = LN_BATCHES // LN_BUFFERS
            for k in range(LN_BUFFERS):
                body(0, k)
            with engine.Fori(1, rounds) as i:
                for k in range(LN_BUFFERS):
                    body(i, k)
            for k in range(LN_BATCHES - rounds * LN_BUFFERS):
                body(rounds, k)

        def first(i):
            return isinstance(i, int) and i == 0

        def wait_table(engine):
            for k in range(LN_BUFFERS):
                engine.wait_ge(t_out[k], 16 * len(range(k, LN_BATCHES, LN_BUFFERS)))

        def inverse_sqrt(engine, wait, y, var, half, work, sem, at, steps=None):
            start = (lambda: engine.tensor_scalar(half, var, EPS, -0.5, ALU.add, ALU.mult),
                     lambda: engine.tensor_scalar(y, var, EPS, None, ALU.add),
                     lambda: engine.tensor_scalar(y.bitcast(I32), y.bitcast(I32), -0.5, float(0x5F3759DF),
                                                  ALU.mult, ALU.add))
            newton = (lambda: engine.tensor_tensor(work, y, y, ALU.mult),
                      lambda: engine.tensor_tensor(work, work, half, ALU.mult))
            if engine is nc.vector:
                newton += (lambda: engine.scalar_tensor_tensor(y, work, 1.5, y, ALU.add, ALU.mult),)
            else:
                newton += (lambda: engine.tensor_scalar(work, work, 1.5, None, ALU.add),
                           lambda: engine.tensor_tensor(y, work, y, ALU.mult))
            for k in steps or range(len(start + NEWTON * newton)):
                (start + NEWTON * newton)[k]().then_inc(sem, 1)
                wait(sem, at + k + 1)

        @block.sync
        def _(sp):
            xb = x.rearrange("(b t p) d -> b p t d", p=P, t=LN_TILES)

            def load_x(i, k):
                if not first(i):
                    sp.wait_ge(feat_ready, (i * LN_BUFFERS + k - LN_BUFFERS + 1) * LN_TILES)
                sp.dma_start(ln_x[k].rearrange("p (t d) -> p t d", d=D),
                             xb[i * LN_BUFFERS + k]).then_inc(x_in[k], 16)

            over_batches(sp, load_x)
            for u in range(SLOTS):
                sp.dma_start(idx[:, u * CHUNKS:(u + 1) * CHUNKS], src[u]).then_inc(idx_in[u], 16)
            for buf, ap in ((group_max_i[:, :], group_max), (dst_i, dst),
                            (router_raw[:, :].rearrange("p (k e) -> p k e", k=HALVES),
                             router_t.rearrange("(k p) e -> p k e", p=P)),
                            (gw_sb[:, :].rearrange("p (k d) -> p k d", k=HALVES),
                             gw.rearrange("(k p) d -> p k d", p=P)),
                            (b1_sb[:, :], b1), (b2_sb[:, :], b2)):
                sp.dma_start(buf, ap).then_inc(consts, 16)
            wait_table(sp)
            for raw, w in ((raw_w1, w1), (raw_w2, w2)):
                sp.dma_start(raw.rearrange("p (k f) -> p k f", f=D),
                             w.rearrange("e (k p) f -> p (e k) f", p=P)).then_inc(weights_in, 16)
            tile, end, unit, limit = (sp.alloc_register(f"sp_{r}") for r in ("tile", "end", "unit", "limit"))

            def load_end():
                i = sp.snap(tile, min_val=0, max_val=TILES)
                sp.reg_mov(end, sp.value_load(last_group[0:1, bass.ds(i, 1)], min_val=0, max_val=GROUPS + 1))

            def lone_wait(sem, value):
                sp.wait_ge(sem, value)
                sp.sem_inc(loads_passed, 1)

            def store_sums(group):
                with sp.While(lambda: sp.snap(end) == group):
                    i = sp.snap(tile, min_val=0, max_val=TILES - 1)
                    lone_wait(parked, i + 2)
                    lone_wait(in_dram, i * 16 + 32)
                    sp.dma_start(park[bass.ds((TILES - 1 - i) * P, P)],
                                 staged[:, bass.ds((i & 1) * D, D)]).then_inc(in_dram, 16)
                    sp.reg_add(tile, tile, 1)
                    load_end()

            def load_pair(m, below):
                half_of = lambda a: a.rearrange("(h p) d -> p h d", p=P)
                lone_wait(base_ready, m + 1)
                sp.dma_start(by_half(x1[:, :]), half_of(x[last_row_pair(below)])).then_inc(x_tile, 16)
                lone_wait(agg_sum, m + 1)
                sp.dma_start(by_half(self_rows[:, :]), half_of(table[last_row_pair(below)])).then_inc(self_tile, 16)
                lone_wait(gnn_done, m + 1)
                sp.dma_start(by_half(agg), half_of(park[last_row_pair(below)])).then_inc(agg_ready, 16)

            def next_unit():
                m = sp.snap(unit, min_val=0, max_val=PAIRS - 1)
                lone_wait(in_dram, m * 32 + 64)
                load_pair(m, PAIRS - 1 - m)
                sp.reg_add(unit, unit, 1)

            sp.wait_ge(ready, 1)
            sp.reg_mov(tile, 0)
            sp.reg_mov(unit, 0)
            load_end()
            with sp.Fori(0, ITERS) as it:
                sp.reg_mov(limit, sp.snap(tile, min_val=0, max_val=TILES) >> 1)
                with sp.If(sp.snap(unit) < sp.snap(limit)):
                    next_unit()
                for u in range(SLOTS):
                    sp.wait_ge(row_in[u], (it + 1) * (16 * CHUNKS))
                    sp.dma_start(idx[:, u * CHUNKS:(u + 1) * CHUNKS],
                                 src[(it + 1) * SLOTS + u]).then_inc(idx_in[u], 16)
                    store_sums(it * SLOTS + u)
            with sp.While(lambda: sp.snap(unit) < PAIRS):
                next_unit()
            load_pair(PAIRS, 0)
            for u in range(SLOTS):
                sp.wait_ge(idx_in[u], (ITERS + 1) * 16)

        @block.gpsimd
        def _(pool):
            pool.iota(node_row[:, :], [[1, P]], base=0, channel_multiplier=0,
                      allow_small_or_imprecise_dtypes=True).then_inc(iotas, 1)
            pool.iota(part_col[:, :], [[0, 1]], base=0, channel_multiplier=1,
                      allow_small_or_imprecise_dtypes=True).then_inc(iotas, 1)
            pool.iota(tile_base[:, 0:TILES + 1], [[-P, TILES + 1]], base=(TILES - 1) * P,
                      channel_multiplier=0, allow_small_or_imprecise_dtypes=True).then_inc(iotas, 1)
            pool.iota(expert_row[:, :], [[1, EXPERTS]], base=0, channel_multiplier=0,
                      allow_small_or_imprecise_dtypes=True).then_inc(iotas, 1)

            def lone_wait(sem, value):
                pool.wait_ge(sem, value)
                pool.sem_inc(pool_passed, 1)

            def ln_scales(i, k):
                b = i * LN_BUFFERS + k
                c = k * LN_TILES
                moments = ln_mv[:, 2 * c:2 * c + 2 * LN_TILES]
                rstd_k, nmr_k = ln_rstd[:, c:c + LN_TILES], ln_nmr[:, c:c + LN_TILES]
                lone_wait(moments_ready, b + 1)
                if not first(i):
                    lone_wait(feat_ready, (b - LN_BUFFERS + 1) * LN_TILES)
                inverse_sqrt(pool, lone_wait, rstd_k, moments[:, 1::2], ln_half[:, :], ln_work[:, :],
                             ln_scale_step, b * (LN_SQRT_STEPS + 2))
                pool.tensor_scalar(rstd_k, rstd_k, FSCALE, None, ALU.mult).then_inc(ln_scale_step, 1)
                pool.tensor_scalar(ln_work[:, :], moments[:, 0::2], -1.0, None, ALU.mult).then_inc(ln_scale_step, 1)
                lone_wait(ln_scale_step, (b + 1) * (LN_SQRT_STEPS + 2))
                pool.tensor_tensor(nmr_k, ln_work[:, :], rstd_k, ALU.mult).then_inc(stats_ready, 1)

            over_batches(pool, ln_scales)
            wait_table(pool)

            def gather(it, u):
                lone_wait(idx_in[u], (it + 1) * 16)
                for j in range(CHUNKS):
                    c = u * CHUNKS + j
                    pool.indirect_dma_start(
                        rows[:, c * 2 * D:(c + 1) * 2 * D], None, table,
                        bass.IndirectOffsetOnAxis(ap=idx[:, c:c + 1], axis=0)).then_inc(row_in[u], 16)

            for u in range(SLOTS):
                gather(0, u)
            with pool.Fori(1, ITERS) as it:
                for u in range(SLOTS):
                    pool.wait_ge(slot_free[u], it)
                    gather(it, u)

        @block.vector
        def _(v):
            n = 0

            def own(ins):
                nonlocal n
                n += 1
                ins.then_inc(set_up, 1)

            own(v.memset(last_group[:, :], GROUPS + 1))
            own(v.memset(ones_col[:, :], 1.0))
            own(v.memset(zero_col[:, :], 0.0))
            own(v.memset(dst_f[:, GROUPS * CHUNKS:], float(FAR)))
            own(v.memset(comb[:, :], 0.0))
            own(v.memset(tok_hi[:, :].bitcast(F32), 0.0))
            own(v.memset(onehot[:, :], 0.0))
            own(v.memset(hid_hi[:, :].bitcast(F32), 0.0))
            v.memset(base[:, :], 0.0).then_inc(y_added, 1)
            v.memset(acc[:, :], 0.0).then_inc(y_added, 1)
            v.memset(hid_lo[:, :].bitcast(F32), 0.0).then_inc(hid_lo_ready, 1)
            v.memset(tok_lo[:, :].bitcast(F32), 0.0).then_inc(tok_lo_ready, 1)
            v.memset(lead[:, :], 0.0).then_inc(base_ready, 1)
            v.memset(scratch[:, :], 0.0).then_inc(parked, 1)
            v.memset(comb_a[:, :], 0.0).then_inc(in_dram, 32)
            v.memset(comb_b[:, :], 0.0).then_inc(stored, 16)
            def lone_wait(sem, value):
                v.wait_ge(sem, value)
                v.sem_inc(vector_passed, 1)

            def moments(i, k):
                b = i * LN_BUFFERS + k
                if not (first(i) and k == 0):
                    v.wait_ge(moments_ready, b)
                v.wait_ge(x_in[k], i * 16 + 16)
                for t in range(LN_TILES):
                    ins = v.bn_stats(stats[:, 6 * t:6 * t + 6], ln_x[k][:, t * D:(t + 1) * D])
                ins.then_inc(ln_step, 1)
                if not first(i):
                    lone_wait(stats_ready, b - LN_BUFFERS + 1)
                lone_wait(ln_step, b + 1)
                at = 2 * k * LN_TILES
                for t in range(LN_TILES):
                    ins = v.bn_aggr(ln_mv[:, at + 2 * t:at + 2 * t + 2], stats[:, 6 * t:6 * t + 6])
                ins.then_inc(moments_ready, 1)

            def low(b, k):
                v.wait_ge(hi_ready, b + 1)
                hi_lo = ln_t[k].rearrange("p (t c) -> p t c", c=2 * D)
                v.tensor_tensor(hi_lo[:, :, D:2 * D], ln_f[k].rearrange("p (t d) -> p t d", d=D),
                                hi_lo[:, :, 0:D], ALU.subtract).then_inc(lo_ready, 1)

            def ln_batch(i, k):
                moments(i, k)
                if not (first(i) and k < 2):
                    low(i * LN_BUFFERS + k - 2, (k - 2) % LN_BUFFERS)

            over_batches(v, ln_batch)
            for b in (LN_BATCHES - 2, LN_BATCHES - 1):
                low(b, b % LN_BUFFERS)

            v.wait_ge(iotas, 4)
            own(v.tensor_scalar(ident[:, :], node_row[:, :], part_col[:, 0:1], None, ALU.is_equal))
            own(v.tensor_scalar(ident16[:, :], node_row[:, :], part_col[:, 0:1], None, ALU.is_equal))
            v.wait_ge(consts, 16 * 6)
            own(v.tensor_copy(group_max_f[:, :], group_max_i[:, :]))
            own(v.tensor_copy(dst_f[:, 0:GROUPS * CHUNKS], dst_i))
            parts = router[:, :].rearrange("p (k s e) -> p k s e", s=2, e=EXPERTS)
            raw = router_raw[:, :].rearrange("p (k e) -> p k e", e=EXPERTS)
            own(v.tensor_copy(parts[:, :, 0, :], raw))
            v.wait_ge(set_up, n)
            own(v.tensor_tensor(parts[:, :, 1, :], raw, parts[:, :, 0, :].bitcast(F32), ALU.subtract))
            for k in range(4):
                own(v.tensor_scalar(reaches[:, k * TILES:(k + 1) * TILES], tile_base[:, 0:TILES],
                                    group_max_f[:, k:k + 1], None, ALU.is_le))
            assert n == SETUP_STEPS
            v.wait_ge(counted, 1)
            own(v.tensor_scalar(last_group[0:1, 0:TILES], ps_g[0:1, 0:TILES], -1.0, None, ALU.add))

            v.wait_ge(set_up, n)
            v.tensor_copy(scratch[:, :], ones_col[:, :]).then_inc(ready, 1)
            wait_table(v)

            step, used, tile, end, unit, limit = (v.alloc_register(f"v_{r}") for r in (
                "step", "used", "tile", "end", "unit", "limit"))

            def one_hot(group, i):
                s = v.snap(step, min_val=0, max_val=GROUPS + TILES + 2)
                v.wait_ge(onehot_free, s + 1)
                at = (s & (RING - 1)) * (CHUNKS * P)
                v.scalar_tensor_tensor(
                    onehot[:, bass.ds(at, CHUNKS * P)].rearrange("p (c n) -> p c n", n=P),
                    node_row[:, :].unsqueeze(1).to_broadcast([P, CHUNKS, P]),
                    tile_base[:, bass.ds(i, 1)],
                    dst_f[:, bass.ds(group * CHUNKS, CHUNKS)].unsqueeze(2).to_broadcast([P, CHUNKS, P]),
                    ALU.add, ALU.is_equal).then_inc(onehot_ready, 1)
                v.reg_add(step, step, 1)

            def low_weights(u):
                raw, hi, lo = ((raw_w1, w1_hi, w1_lo), (raw_w2, w2_hi, w2_lo))[u // 4]
                at = slice(u % 4 * (WCOLS // 4), (u % 4 + 1) * (WCOLS // 4))
                v.wait_ge(w_hi, u // 4 + 1)
                v.tensor_tensor(lo[:, at], raw[:, at], hi[:, at].bitcast(F32), ALU.subtract).then_inc(w_lo, 1)

            def tile_value():
                return v.snap(tile, min_val=0, max_val=TILES)

            def load_end():
                v.reg_mov(end, v.value_load(last_group[0:1, bass.ds(tile_value(), 1)], min_val=0, max_val=GROUPS + 1))

            def prepare(group):
                one_hot(group, tile_value())
                with v.If(v.snap(end) == group):
                    one_hot(group, v.snap(tile, min_val=0, max_val=TILES - 1) + 1)

            def walk(group):
                v.reg_add(used, used, 1)
                with v.While(lambda: v.snap(end) == group):
                    v.wait_ge(onehot_free, v.snap(used, min_val=1, max_val=GROUPS + TILES + 2) + RING)
                    i = v.snap(tile, min_val=0, max_val=TILES - 1)
                    v.wait_ge(in_dram, i * 16 + 16)
                    at = (i & 1) * 512
                    v.tensor_reduce(staged[:, bass.ds((i & 1) * D, D)],
                                    sums[:, bass.ds(at, 2 * D)].rearrange("p (h d) -> p d h", h=2),
                                    mybir.AxisListType.X, ALU.add).then_inc(parked, 1)
                    v.reg_add(tile, tile, 1)
                    v.reg_add(used, used, 1)
                    load_end()
                    with v.If(v.snap(end) == group):
                        one_hot(group, v.snap(tile, min_val=0, max_val=TILES - 1) + 1)

            def routed(ins, m, k, alone=False):
                ins.then_inc(route, 1)
                (lone_wait if alone else v.wait_ge)(route, m * ROUTE_STEPS + k)

            def read_logits(m):
                v.wait_ge(logits_done, m + 1)
                routed(v.tensor_reduce(logit[:, :].rearrange("p (h e) -> p h e", h=2),
                                       ps_t[:, 0:4 * EXPERTS].rearrange("p (h s e) -> p h e s", h=2, s=2),
                                       mybir.AxisListType.X, ALU.add), m, 1, alone=True)

            def top_experts(m):
                v.max(top[:, 0:8], logit[:, 0:EXPERTS])
                routed(v.max(top[:, 8:16], logit[:, EXPERTS:]), m, 2, alone=True)
                v.max_index(top_i[:, 0:8], top[:, 0:8], logit[:, 0:EXPERTS])
                routed(v.max_index(top_i[:, 8:16], top[:, 8:16], logit[:, EXPERTS:]), m, 3)
                by_tile = top[:, :].rearrange("p (h e) -> p h e", h=2)
                v.tensor_tensor(lead[:, :].unsqueeze(2), by_tile[:, :, 0:1], by_tile[:, :, 1:2],
                                ALU.subtract).then_inc(lead_ready, 1)
                routed(v.tensor_copy(top_f[:, :].rearrange("p (h e) -> p h e", h=2),
                                     top_i[:, :].rearrange("p (h e) -> p h e", h=2)[:, :, 0:2]), m, 4)

            def combine_weights(m):
                v.wait_ge(tanh_ready, m + 1)
                v.tensor_scalar(wgt[:, 0:4:2], tanh[:, :], 0.5, 0.5, ALU.mult, ALU.add)
                routed(v.tensor_scalar(wgt[:, 1:4:2], tanh[:, :], -0.5, 0.5, ALU.mult, ALU.add), m, 5)
                for h in (0, 1):
                    for k, part_of in enumerate((comb_a, comb_b)):
                        c = 2 * h + k
                        ins = v.tensor_scalar(part_of[:, h * EXPERTS:(h + 1) * EXPERTS], expert_row[:, :],
                                              top_f[:, c:c + 1], wgt[:, c:c + 1], ALU.is_equal, ALU.mult)
                routed(ins, m, 6)
                routed(v.tensor_tensor(comb[:, :], comb_a[:, :], comb_b[:, :], ALU.add), m, 7)

            def hid_low(m, e):
                at = slice((e & 1) * D2, (e & 1) * D2 + D2)
                v.wait_ge(hid_hi_ready, m * EXPERTS + e + 1)
                v.tensor_tensor(hid_lo[:, at], gel[:, at], hid_hi[:, at].bitcast(F32),
                                ALU.subtract).then_inc(hid_lo_ready, 1)

            def add_output(m, u):
                e = (u - 2) % EXPERTS
                v.wait_ge(y_done, m * EXPERTS + u + 1)
                v.wait_ge(y_added, m * EXPERTS + u + 2)
                if u == 5:
                    v.wait_ge(bias_added, m + 1)
                if e == EXPERTS - 1:
                    v.wait_ge(stored, m * 16 + 16)
                so_far = base if e == 0 else acc
                into = acc_out if e == EXPERTS - 1 else acc
                for h in (0, 1):
                    at = slice(h * D, (h + 1) * D)
                    ins = v.scalar_tensor_tensor(into[:, at], ps_y[e & 1][:, at],
                                                 comb[:, h * EXPERTS + e:h * EXPERTS + e + 1], so_far[:, at],
                                                 ALU.mult, ALU.add)
                ins.then_inc(y_added, 1)

            def add_bias(m):
                v.wait_ge(bias_done, m + 1)
                v.wait_ge(y_added, m * EXPERTS + 7)
                v.tensor_tensor(acc[:, :], acc[:, :], ps_g[:, :], ALU.add).then_inc(bias_added, 1)

            def residual(m):
                v.wait_ge(gnn_done, m + 2)
                v.wait_ge(x_tile, m * 16 + 16)
                v.scalar_tensor_tensor(x1[:, :], ps_g[:, :], 0.0, x1[:, :],
                                       ALU.max, ALU.add).then_inc(front, 1)
                v.wait_ge(front, m * FRONT_STEPS + 1)
                for h in (0, 1):
                    ins = v.bn_stats(stats[:, 6 * h:6 * h + 6], x1[:, h * D:(h + 1) * D])
                ins.then_inc(front, 1)
                lone_wait(front, m * FRONT_STEPS + 2)
                for h in (0, 1):
                    ins = v.bn_aggr(mv[:, 2 * h:2 * h + 2], stats[:, 6 * h:6 * h + 6])
                ins.then_inc(front, 1)

            def scale(m, steps):
                v.wait_ge(front, m * FRONT_STEPS + 3 + steps.start)
                inverse_sqrt(v, v.wait_ge, rstd[:, :], mv[:, 1:4:2], half[:, :], work[:, :],
                             front, m * FRONT_STEPS + 3, steps)

            def normalize(m):
                for h in (0, 1):
                    at = slice(h * D, (h + 1) * D)
                    ins = v.tensor_scalar(normed[:, at], x1[:, at], mv[:, 2 * h:2 * h + 1], rstd[:, h:h + 1],
                                          ALU.subtract, ALU.mult)
                ins.then_inc(normed_ready, 1)

            def part(m, u):
                if u == 1:
                    read_logits(m)
                if u == 2:
                    combine_weights(m)
                if u == 5:
                    add_bias(m)
                add_output(m, u)
                if u == 1:
                    top_experts(m)
                if u == 3:
                    residual(m)
                if u == 4:
                    v.wait_ge(comb_td, m + 1)
                    v.tensor_copy(comb_t[:, :], ps_t[0:EXPERTS, 0:P2]).then_inc(comb_tr, 1)
                    scale(m, range(0, 5))
                if u == 5:
                    scale(m, range(5, 9))
                if u == 6:
                    scale(m, range(9, SQRT_STEPS))
                    normalize(m)
                if u == EXPERTS - 1:
                    v.wait_ge(normed_ready, m + 1)
                    v.tensor_tensor(base[:, :], x1[:, :], normed, ALU.add).then_inc(base_ready, 1)
                    v.wait_ge(tok_hi_ready, m + 1)
                    v.tensor_tensor(tok_lo[:, :], ps_t[:, :], tok_hi[:, :].bitcast(F32),
                                    ALU.subtract).then_inc(tok_lo_ready, 1)
                hid_low(m, u)

            def unit_value():
                return v.snap(unit, min_val=0, max_val=UNITS - 1)

            v.reg_mov(step, 0)
            v.reg_mov(tile, 0)
            v.reg_mov(unit, 0)
            v.reg_mov(used, 0)
            load_end()
            prepare(0)
            for u in range(SLOTS):
                walk(u)
                prepare(u + 1)
                low_weights(u)
            with v.Fori(1, ITERS) as it:
                v.reg_mov(limit, tile_value() >> 1)
                with v.If(v.snap(unit) < v.snap(limit)):
                    m = unit_value()
                    for u in range(SLOTS):
                        walk(it * SLOTS + u)
                        prepare(it * SLOTS + u + 1)
                        part(m, u)
                    v.reg_add(unit, unit, 1)
                with v.Else():
                    for u in range(SLOTS):
                        walk(it * SLOTS + u)
                        prepare(it * SLOTS + u + 1)
            with v.While(lambda: v.snap(unit) < UNITS):
                for u in range(EXPERTS):
                    part(unit_value(), u)
                v.reg_add(unit, unit, 1)
            for u in (0, 1):
                add_output(UNITS, u)

        @block.tensor
        def _(pe):
            pe.wait_ge(set_up, SETUP_STEPS)
            for k in range(4):
                mm = pe.matmul(ps_g[0:1, 0:TILES], ones_col[:, :], reaches[:, k * TILES:(k + 1) * TILES],
                               start=(k == 0), stop=(k == 3))
            mm.then_inc(counted, 1)
            pe.wait_ge(ready, 1)
            for done in (agg_sum, gnn_done):
                pe.matmul(ps_t[:, 0:P], onehot[:, 0:P], onehot[:, 0:P], start=True, stop=True).then_inc(done, 1)
            for k in (0, 1):
                mm = pe.matmul(ps_y[k][:, :], onehot[:, 0:P], onehot[:, 0:512], start=True, stop=True)
            mm.then_inc(y_done, 1)
            for k in (0, 1):
                mm = pe.matmul(sums[:, 512 * k:512 * k + 512], onehot[:, 0:P], onehot[:, 0:512],
                               start=True, stop=True)
            mm.then_inc(onehot_free, RING)

            step1, tile1, end, next_end, at, bank, unit, limit = (pe.alloc_register(f"pe_{r}") for r in (
                "step1", "tile1", "end", "next_end", "at", "bank", "unit", "limit"))
            AT = RING * CHUNKS * P

            def load_end(tile):
                return pe.value_load(last_group[0:1, bass.ds(tile, 1)], min_val=0, max_val=GROUPS + 1)

            def sum_group(u, first):
                a = pe.snap(at, min_val=0, max_val=AT - CHUNKS * P)
                b = pe.snap(bank, min_val=0, max_val=512)
                pe.wait_ge(onehot_ready, pe.snap(step1, min_val=1, max_val=GROUPS + TILES + 3))
                for j in range(CHUNKS):
                    c = u * CHUNKS + j
                    mm = pe.matmul(sums[:, bass.ds(b, 2 * D)], onehot[:, bass.ds(a + j * P, P)],
                                   rows[:, c * 2 * D:(c + 1) * 2 * D], start=(first and j == 0),
                                   stop=False, skip_group_check=True)
                mm.then_inc(onehot_free, 1)
                pe.reg_add(step1, step1, 1)
                pe.reg_add(at, at, CHUNKS * P)
                pe.reg_alu(at, at, AT - 1, ALU.bitwise_and)

            def walk(it, u):
                pe.wait_ge(row_in[u], (it + 1) * (16 * CHUNKS))
                sum_group(u, False)
                with pe.While(lambda: pe.snap(end) == it * SLOTS + u):
                    pe.reg_mov(end, next_end)
                    pe.reg_alu(bank, bank, 512, ALU.bitwise_xor)
                    pe.wait_ge(parked, pe.snap(tile1, min_val=1, max_val=TILES + 1))
                    sum_group(u, True)
                    pe.reg_add(tile1, tile1, 1)
                    pe.reg_mov(next_end, load_end(pe.snap(tile1, min_val=1, max_val=TILES + 1)))
                pe.matmul(sums[0:1, bass.ds(pe.snap(bank, min_val=0, max_val=512), 2)], zero_col[:, 0:1],
                          ident16[:, 0:2], start=False, stop=False, skip_group_check=True).then_inc(slot_free[u], 1)

            def hidden(m, e):
                if e == 0:
                    pe.wait_ge(tok_lo_ready, m + 1)
                for f in range(HALVES):
                    n = 0
                    for w, t in ((w1_hi, tok_hi), (w1_hi, tok_lo), (w1_lo, tok_hi)):
                        for k in range(HALVES):
                            mm = pe.matmul(ps_h[e & 1][:, f * P2:(f + 1) * P2],
                                           w[:, wcol(e, k, f):wcol(e, k, f) + P], t[:, k * P2:(k + 1) * P2],
                                           start=(n == 0), stop=(n == 3 * HALVES - 1))
                            n += 1
                mm.then_inc(h_done, 1)

            def output(m, u):
                e = (u - 1) % EXPERTS
                pe.wait_ge(hid_lo_ready, m * EXPERTS + u + 1)
                pe.wait_ge(y_added, m * EXPERTS + u + 2)
                for h in (0, 1):
                    n = 0
                    for t, w in ((hid_hi, w2_hi), (hid_hi, w2_lo), (hid_lo, w2_hi)):
                        for k in range(HALVES):
                            at = (e & 1) * D2 + k * P2 + h * P
                            mm = pe.matmul(ps_y[e & 1][:, h * D:(h + 1) * D], t[:, at:at + P],
                                           w[:, wcol(e, k):wcol(e, k) + D],
                                           start=(n == 0), stop=(n == 3 * HALVES - 1))
                            n += 1
                mm.then_inc(y_done, 1)

            def transpose_agg(m):
                pe.wait_ge(route, m * ROUTE_STEPS + 1)
                pe.wait_ge(agg_ready, m * 16 + 16)
                pe.wait_ge(self_tile, m * 16 + 16)
                for k in range(HALVES):
                    for h in (0, 1):
                        o = ps_t[:, k * P2 + h * P:k * P2 + (h + 1) * P]
                        at = h * D2 + k * P
                        pe.matmul(o, agg[:, h * D + k * P:h * D + (k + 1) * P], ident[:, :], start=True, stop=False)
                        pe.matmul(o, self_rows[:, at:at + P], ident16[:, :], start=False, stop=False)
                        mm = pe.matmul(o, self_rows[:, at + D:at + D + P], ident16[:, :],
                                       start=False, stop=True)
                mm.then_inc(agg_sum, 1)

            def graph_product(m):
                pe.wait_ge(agg_t, m + 1)
                for h in (0, 1):
                    for k in range(HALVES):
                        at = k * P2 + h * P
                        mm = pe.matmul(ps_g[:, h * D:(h + 1) * D], agg[:, at:at + P], gw_sb[:, k * D:(k + 1) * D],
                                       start=(k == 0), stop=(k == HALVES - 1))
                mm.then_inc(gnn_done, 1)

            def logits(m):
                for h in (0, 1):
                    for t, cols in ((tok_hi, 2 * EXPERTS), (tok_lo, EXPERTS)):
                        for k in range(HALVES):
                            at = k * P2 + h * P
                            mm = pe.matmul(ps_t[:, 2 * h * EXPERTS:2 * h * EXPERTS + cols], t[:, at:at + P],
                                           router[:, 2 * k * EXPERTS:2 * k * EXPERTS + cols],
                                           start=(t is tok_hi and k == 0), stop=(t is tok_lo and k == HALVES - 1),
                                           skip_group_check=True)
                mm.then_inc(logits_done, 1)

            def part(m, u):
                if u == EXPERTS - 1:
                    pe.wait_ge(normed_ready, m + 1)
                    for k in range(HALVES):
                        for h in (0, 1):
                            mm = pe.transpose(ps_t[:, k * P2 + h * P:k * P2 + (h + 1) * P],
                                              normed[:, h * D + k * P:h * D + (k + 1) * P], ident[:, :])
                    mm.then_inc(tok_t, 1)
                hidden(m, u)
                output(m, u)
                if u == 0:
                    logits(m)
                if u == 1:
                    transpose_agg(m)
                if u == 2:
                    graph_product(m)
                if u == 3:
                    pe.wait_ge(route, (m + 1) * ROUTE_STEPS)
                    for h in (0, 1):
                        mm = pe.transpose(ps_t[0:EXPERTS, h * P:(h + 1) * P],
                                          comb[:, h * EXPERTS:(h + 1) * EXPERTS], ident[:, :])
                    mm.then_inc(comb_td, 1)
                if u == 4:
                    pe.wait_ge(front, m * FRONT_STEPS + 1)
                    pe.wait_ge(comb_tr, m + 1)
                    for h in (0, 1):
                        mm = pe.matmul(ps_g[:, h * D:(h + 1) * D], comb_t[:, h * P:(h + 1) * P], b2_sb[:, :],
                                       start=True, stop=True)
                    mm.then_inc(bias_done, 1)

            def unit_value():
                return pe.snap(unit, min_val=0, max_val=UNITS - 1)

            for register, value in ((step1, 1), (tile1, 1), (at, 0), (bank, 0), (unit, 0)):
                pe.reg_mov(register, value)
            pe.reg_mov(end, load_end(0))
            pe.reg_mov(next_end, load_end(1))
            for u in range(SLOTS):
                walk(0, u)
            pe.wait_ge(w_lo, 8)
            with pe.Fori(1, ITERS) as it:
                pe.reg_mov(limit, (pe.snap(tile1, min_val=1, max_val=TILES + 1) - 1) >> 1)
                with pe.If(pe.snap(unit) < pe.snap(limit)):
                    m = unit_value()
                    for u in range(SLOTS):
                        walk(it, u)
                        part(m, u)
                    pe.reg_add(unit, unit, 1)
                with pe.Else():
                    for u in range(SLOTS):
                        walk(it, u)
            with pe.While(lambda: pe.snap(unit) < UNITS):
                for u in range(EXPERTS):
                    part(unit_value(), u)
                pe.reg_add(unit, unit, 1)
            output(UNITS, 0)

        @block.scalar
        def _(act):
            tb = table.rearrange("(b t p) c -> b p t c", p=P, t=LN_TILES)

            def features(i, k):
                b = i * LN_BUFFERS + k
                act.wait_ge(stats_ready, b + 1)
                if not first(i):
                    act.wait_ge(lo_ready, b - LN_BUFFERS + 1)
                for t in range(LN_TILES):
                    c = k * LN_TILES + t
                    act.activation(ln_f[k][:, t * D:(t + 1) * D], ln_x[k][:, t * D:(t + 1) * D], ACT.Identity,
                                   bias=ln_nmr[:, c:c + 1], scale=ln_rstd[:, c:c + 1]).then_inc(feat_ready, 1)

            def store(b, k):
                act.wait_ge(lo_ready, b + 1)
                act.dma_start(tb[b], ln_t[k].rearrange("p (t c) -> p t c", c=2 * D)).then_inc(t_out[k], 16)

            def ln_batch(i, k):
                b = i * LN_BUFFERS + k
                features(i, k)
                if not (first(i) and k == 0):
                    store(b - 1, (k - 1) % LN_BUFFERS)
                if not first(i):
                    act.wait_ge(t_out[k], i * 16)
                act.wait_ge(feat_ready, (b + 1) * LN_TILES)
                act.activation(ln_t[k].rearrange("p (t c) -> p t c", c=2 * D)[:, :, 0:D],
                               ln_f[k].rearrange("p (t d) -> p t d", d=D), ACT.Copy).then_inc(hi_ready, 1)

            act.wait_ge(set_up, 2)
            act.activation(scratch_act[:, :], ones_col[:, :], ACT.Gelu)
            over_batches(act, ln_batch)
            store(LN_BATCHES - 1, (LN_BATCHES - 1) % LN_BUFFERS)
            for k, (raw, hi) in enumerate(((raw_w1, w1_hi), (raw_w2, w2_hi))):
                act.wait_ge(weights_in, 32)
                act.activation(hi[:, :], raw, ACT.Copy).then_inc(w_hi, 1)
            wait_table(act)
            act.wait_ge(ready, 1)

            def unit(m):
                for e in range(EXPERTS):
                    act.wait_ge(h_done, m * EXPERTS + e + 1)
                    at = (e & 1) * D2
                    if e == EXPERTS - 1:
                        act.wait_ge(tok_t, m + 1)
                        act.activation(tok_hi[:, :], ps_t[:, :], ACT.Copy).then_inc(tok_hi_ready, 1)
                    for f in range(HALVES):
                        g = act.activation(gel[:, at + f * P2:at + (f + 1) * P2],
                                           ps_h[e & 1][:, f * P2:(f + 1) * P2], ACT.Gelu,
                                           bias=b1_sb[:, e * HALVES + f:e * HALVES + f + 1])
                    g.then_inc(gel_ready, 1)
                    act.wait_ge(gel_ready, m * EXPERTS + e + 1)
                    act.activation(hid_hi[:, at:at + D2], gel[:, at:at + D2], ACT.Copy).then_inc(hid_hi_ready, 1)
                    if e == 1:
                        act.wait_ge(lead_ready, m + 1)
                        act.activation(tanh[:, :], lead[:, :], ACT.Tanh, scale=0.5).then_inc(tanh_ready, 1)
                        act.wait_ge(agg_sum, m + 2)
                        act.activation(agg, ps_t[:, :], ACT.Copy, scale=1.0 / FSCALE).then_inc(agg_t, 1)
                    if e == 2:
                        store_result(m)

            def store_result(m):
                act.wait_ge(y_added, m * EXPERTS + 4)
                act.dma_start(out[last_row_pair(UNITS - m)].rearrange("(h p) d -> p h d", p=P),
                              by_half(acc_out[:, :])).then_inc(stored, 16)

            with act.Fori(0, UNITS) as m:
                unit(m)
            store_result(UNITS)
            act.wait_ge(stored, (UNITS + 2) * 16)


def kernel(**inputs):
    import numpy as np
    from concourse import bacc
    from concourse.bass_utils import run_bass_kernel_spmd

    a = {k: np.asarray(v) for k, v in inputs.items()}
    padded = GROUPS * GROUP
    src = np.zeros(padded, np.int32)
    dst = np.full(padded, FAR, np.int32)
    src[padded - EDGES:] = a["src"][::-1]
    dst[padded - EDGES:] = a["dst"][::-1]
    group_max = np.full(4 * P, -1, np.int32)
    group_max[:GROUPS] = dst[::GROUP]
    x = np.zeros((ROWS, D), np.float32)
    x[:NODES] = a["x"]
    arrays = {
        "x": x,
        "src": np.ascontiguousarray(np.concatenate([src, np.zeros(SLOTS * GROUP, np.int32)]).reshape(GROUPS + SLOTS, P, CHUNKS)),
        "dst": np.ascontiguousarray(dst.reshape(GROUPS, P, CHUNKS).transpose(1, 0, 2).reshape(P, GROUPS * CHUNKS)),
        "group_max": np.ascontiguousarray(group_max.reshape(4, P).T),
        "gw": a["L0_gnn_weight1"],
        "router": np.ascontiguousarray(a["L0_ffn_router_w"].T),
        "w1": a["L0_ffn_w1"],
        "b1": np.ascontiguousarray(a["L0_ffn_b1"].reshape(EXPERTS, HALVES, P).transpose(2, 0, 1).reshape(P, EXPERTS * HALVES)),
        "w2": a["L0_ffn_w2"],
        "b2": a["L0_ffn_b2"],
    }
    nc = bacc.Bacc("TRN2", target_bir_lowering=False, num_devices=1)
    args = [nc.dram_tensor(f"in_{n}", v.shape, mybir.dt.from_np(v.dtype), kind="ExternalInput").ap()
            for n, v in arrays.items()]
    out = nc.dram_tensor("out_0", (ROWS + 2 * P2, D), F32, kind="ExternalOutput").ap()
    build(nc, *args, out)
    r = run_bass_kernel_spmd(nc, [{f"in_{n}": v for n, v in arrays.items()}], core_ids=[0])
    return r.results[0]["out_0"][:NODES]
```

```python
import concourse.bass as bass
import concourse.mybir as mybir
from concourse.alu_op_type import AluOpType as ALU

ACT = mybir.ActivationFunctionType
F32, F32R, F16 = mybir.dt.float32, mybir.dt.float32r, mybir.dt.float16
I32, U32 = mybir.dt.int32, mybir.dt.uint32

P = 128
D = 256
HALVES = D // P
NODES, EDGES, EXPERTS = 12500, 200000, 8
TILES = -(-NODES // P)
ROWS = TILES * P
CHUNKS = 4
GROUP = CHUNKS * P
SLOTS = 8
ITERS = -(-EDGES // (GROUP * SLOTS))
GROUPS = ITERS * SLOTS
RING = 4
PAIRS = TILES // 2
UNITS = PAIRS + 1
D2, P2 = 2 * D, 2 * P
assert SLOTS == EXPERTS
LN_TILES = 7
LN_BATCHES = TILES // LN_TILES
LN_BUFFERS = 4
PREFETCH = 5
MAXES = 2 * D
EPS = 1e-5
FSCALE = 1024.0
FAR = 1 << 20
SETUP_STEPS = 14
NEWTON = 3
SQRT_STEPS, LN_SQRT_STEPS = 3 + 3 * NEWTON, 3 + 4 * NEWTON
ROUTE_STEPS, FRONT_STEPS = 7, 3 + SQRT_STEPS


def build(nc, x, src, dst, group_max, gw, router_t, w1, b1, w2, b2, out):
    table = nc.dram_tensor("feature_table", (ROWS, 2 * D), F16, kind="Internal").ap()
    park = nc.dram_tensor("edge_sums", (ROWS, D), F32, kind="Internal").ap()
    WCOLS = EXPERTS * HALVES * D

    from contextlib import ExitStack
    with ExitStack() as stack:
        def sbuf(name, cols, dtype=F32, parts=P):
            return stack.enter_context(nc.sbuf_tensor(name, [parts, cols], dtype))

        def psum(name, cols=512):
            return stack.enter_context(nc.psum_tensor(name, [P, cols], F32))

        def sem(name):
            return stack.enter_context(nc.semaphore(name))

        w1_hi, w1_lo = sbuf("w1_hi", WCOLS, F32R), sbuf("w1_lo", WCOLS, F32R)
        w2_hi, w2_lo = sbuf("w2_hi", WCOLS, F32R), sbuf("w2_lo", WCOLS, F32R)
        gw_sb = sbuf("gw_sb", HALVES * D)
        router = sbuf("router", 2 * HALVES * EXPERTS, F32R)
        router_raw = sbuf("router_raw", HALVES * EXPERTS)
        b1_sb = sbuf("b1_sb", EXPERTS * HALVES)
        b2_sb = sbuf("b2_sb", D, F32, EXPERTS)
        dst_f = sbuf("dst_f", (GROUPS + 1) * CHUNKS)
        tile_base = sbuf("tile_base", TILES + 2)
        tile_start = sbuf("tile_start", 1)
        ends = sbuf("ends", MAXES, I32, 1)
        node_row = sbuf("node_row", P, F16)
        part_col = sbuf("part_col", 1)
        ident, ident16 = sbuf("ident", P), sbuf("ident16", P, F16)
        expert_row = sbuf("expert_row", EXPERTS)
        scratch_act = sbuf("scratch_act", 1)
        ones_col = sbuf("ones_col", 1)
        idx = sbuf("idx", SLOTS * CHUNKS, I32)
        onehot = sbuf("onehot", RING * CHUNKS * P, F16)
        x1, self_rows = sbuf("x1", D2), sbuf("self_rows", 2 * D2, F16)
        base = sbuf("base", D2)
        tok_hi, tok_lo = sbuf("tok_hi", D2, F32R), sbuf("tok_lo", D2, F32R)
        hid_hi, hid_lo = sbuf("hid_hi", 2 * D2, F32R), sbuf("hid_lo", 2 * D2, F32R)
        acc, acc_out = sbuf("acc", D2), sbuf("acc_out", D2)
        stats, mv = sbuf("stats", 6 * LN_TILES), sbuf("mv", 4)
        half, work, rstd = sbuf("half", 2), sbuf("work", 2), sbuf("rstd", 2)
        ln_mv, ln_rstd, ln_nmr = (sbuf(n, 2 * LN_BUFFERS * LN_TILES) for n in ("ln_mv", "ln_rstd", "ln_nmr"))
        ln_half, ln_work = sbuf("ln_half", LN_TILES), sbuf("ln_work", LN_TILES)
        logit = sbuf("logit", 2 * EXPERTS)
        top, top_i, top_f = sbuf("top", 16), sbuf("top_i", 16, U32), sbuf("top_f", 4)
        lead, tanh, wgt, scratch = sbuf("lead", 2), sbuf("tanh", 2), sbuf("wgt", 4), sbuf("scratch", 1)
        comb_a, comb_b, comb = (sbuf(n, 2 * EXPERTS) for n in ("comb_a", "comb_b", "comb"))
        comb_t = sbuf("comb_t", P2, F32, EXPERTS)
        LN = LN_TILES * D
        B = LN_BUFFERS
        arena = sbuf("arena", 3 * B * LN + GROUPS * CHUNKS)
        ln_x = [arena[:, k * LN:(k + 1) * LN] for k in range(B)]
        ln_f = [arena[:, k * LN:(k + 1) * LN] for k in range(B, 2 * B)]
        ln_t = [arena[:, k * LN:(k + 1) * LN].bitcast(F16) for k in range(2 * B, 3 * B)]
        dst_i = arena[:, 3 * B * LN:].bitcast(I32)
        group_max_i, group_max_f = x1[:, :].bitcast(I32), acc_out[:, :]
        reaches, reached = self_rows[:, :].bitcast(F32), acc_out[0:1, :]
        rows = arena[:, 0:SLOTS * CHUNKS * D].bitcast(F16)
        at = SLOTS * CHUNKS * D
        gel = arena[:, at:at + 2 * D2]
        agg = arena[:, at + 2 * D2:at + 3 * D2]
        normed = arena[:, at + 3 * D2:at + 4 * D2]
        staged = arena[:, at + 4 * D2:at + 5 * D2]
        at += 5 * D2
        raw_w1, raw_w2 = arena[:, at:at + WCOLS], arena[:, at + WCOLS:at + 2 * WCOLS]
        assert at + 2 * WCOLS <= 3 * B * LN
        sums = psum("sums", 1024)
        ps_h = [psum("ps_h_even"), psum("ps_h_odd")]
        ps_y = [psum("ps_y_even"), psum("ps_y_odd")]
        ps_t = psum("ps_t")
        ps_g = psum("ps_g")
        x_in = [sem(f"ln_x_loaded_{k}") for k in range(LN_BUFFERS)]
        t_out = [sem(f"table_stored_{k}") for k in range(LN_BUFFERS)]
        stats_ready, feat_ready, hi_ready, lo_ready = (sem(n) for n in (
            "ln_scale_ready", "ln_feature_ready", "ln_hi_ready", "ln_lo_ready"))
        ln_step, moments_ready, ln_scale_step = (sem(n) for n in (
            "ln_vector_step", "ln_moments_ready", "ln_scale_step"))
        consts, weights_in, iotas = sem("small_inputs_loaded"), sem("expert_weights_loaded"), sem("iotas_ready")
        set_up, counted = sem("vector_setup_step"), sem("group_counts_summed")
        w_hi, w_lo = sem("weight_hi_ready"), sem("weight_lo_ready")
        ready = sem("vector_setup_done")
        vector_passed, pool_passed, loads_passed = (sem(n) for n in (
            "vector_wait_passed", "pool_wait_passed", "loads_wait_passed"))
        idx_in = [sem(f"indices_loaded_{u}") for u in range(SLOTS)]
        row_in = [sem(f"rows_gathered_{u}") for u in range(SLOTS)]
        slot_free = [sem(f"slot_free_{u}") for u in range(SLOTS)]
        onehot_ready, onehot_free, parked = sem("onehot_ready"), sem("onehot_free"), sem("tile_parked")
        in_dram = sem("sum_stored")
        x_tile, self_tile, stored = sem("x_tile_loaded"), sem("self_rows_loaded"), sem("tile_stored")
        agg_ready, agg_added, agg_sum, agg_t = sem("agg_loaded"), sem("self_rows_added"), sem("agg_transposed_sum"), sem("agg_transposed")
        gnn_done, front, normed_ready, base_ready = (sem(n) for n in (
            "graph_product_done", "front_vector_step", "tokens_normed", "base_ready"))
        tok_t, tok_hi_ready, tok_lo_ready = sem("tokens_transposed"), sem("token_hi_ready"), sem("token_lo_ready")
        logits_done, route = sem("logits_done"), sem("route_vector_step")
        lead_ready, tanh_ready = sem("lead_ready"), sem("tanh_of_lead_ready")
        comb_td, comb_tr, bias_done, bias_added = (sem(n) for n in (
            "combine_transposed", "combine_transpose_copied", "bias_sum_done", "bias_sum_added"))
        h_done, gel_ready, hid_hi_ready, hid_lo_ready = (sem(n) for n in (
            "hidden_done", "gelu_ready", "hidden_hi_ready", "hidden_lo_ready"))
        y_done, y_added = sem("expert_output_done"), sem("expert_output_added")
        block = stack.enter_context(nc.Block())

        def wcol(e, k, f=0):
            return (e * HALVES + k) * D + f * P

        def last_row_pair(pairs):
            return bass.ds(pairs * P2, P2)

        def by_half(ap):
            return ap.rearrange("p (h d) -> p h d", h=2)

        def over_batches(engine, body):
            rounds = LN_BATCHES // LN_BUFFERS
            for k in range(LN_BUFFERS):
                body(0, k)
            with engine.Fori(1, rounds) as i:
                for k in range(LN_BUFFERS):
                    body(i, k)
            for k in range(LN_BATCHES - rounds * LN_BUFFERS):
                body(rounds, k)

        def first(i):
            return isinstance(i, int) and i == 0

        def end_counts(engine, name):
            count = [engine.alloc_register(f"{name}_ends_{u}") for u in range(SLOTS)]

            def load(it):
                engine.reg_load(count, ends[0:1, bass.ds(it * SLOTS, SLOTS)])

            def left(u):
                return engine.snap(count[u], min_val=0, max_val=TILES)

            return count, load, left

        def wait_table(engine):
            for k in range(LN_BUFFERS):
                engine.wait_ge(t_out[k], 16 * len(range(k, LN_BATCHES, LN_BUFFERS)))

        def inverse_sqrt(engine, wait, y, var, half, work, sem, at, scale=1.0, steps=None):
            start = (lambda: engine.tensor_scalar(half, var, EPS, -0.5 / scale ** 2, ALU.add, ALU.mult),
                     lambda: engine.tensor_scalar(y, var, EPS, 1 / scale ** 2, ALU.add, ALU.mult),
                     lambda: engine.tensor_scalar(y.bitcast(I32), y.bitcast(I32), -0.5, float(0x5F3759DF),
                                                  ALU.mult, ALU.add))
            newton = (lambda: engine.tensor_tensor(work, y, y, ALU.mult),
                      lambda: engine.tensor_tensor(work, work, half, ALU.mult))
            if engine is nc.vector:
                newton += (lambda: engine.scalar_tensor_tensor(y, work, 1.5, y, ALU.add, ALU.mult),)
            else:
                newton += (lambda: engine.tensor_scalar(work, work, 1.5, None, ALU.add),
                           lambda: engine.tensor_tensor(y, work, y, ALU.mult))
            for k in steps or range(len(start + NEWTON * newton)):
                (start + NEWTON * newton)[k]().then_inc(sem, 1)
                wait(sem, at + k + 1)

        @block.sync
        def _(sp):
            xb = x.rearrange("(b t p) d -> b p t d", p=P, t=LN_TILES)

            def load_x(i, k):
                if not first(i):
                    sp.wait_ge(feat_ready, (i * LN_BUFFERS + k - LN_BUFFERS + 1) * LN_TILES)
                sp.dma_start(ln_x[k].rearrange("p (t d) -> p t d", d=D),
                             xb[i * LN_BUFFERS + k]).then_inc(x_in[k], 16)

            over_batches(sp, load_x)
            for u in range(SLOTS):
                sp.dma_start(idx[:, u * CHUNKS:(u + 1) * CHUNKS], src[u]).then_inc(idx_in[u], 16)
            for buf, ap in ((group_max_i, group_max), (dst_i, dst),
                            (router_raw[:, :].rearrange("p (k e) -> p k e", k=HALVES),
                             router_t.rearrange("(k p) e -> p k e", p=P)),
                            (gw_sb[:, :].rearrange("p (k d) -> p k d", k=HALVES),
                             gw.rearrange("(k p) d -> p k d", p=P)),
                            (b1_sb[:, :], b1), (b2_sb[:, :], b2)):
                sp.dma_start(buf, ap).then_inc(consts, 16)
            wait_table(sp)
            for raw, w in ((raw_w1, w1), (raw_w2, w2)):
                sp.dma_start(raw.rearrange("p (k f) -> p k f", f=D),
                             w.rearrange("e (k p) f -> p (e k) f", p=P)).then_inc(weights_in, 16)
            tile, unit, summed, limit = (sp.alloc_register(f"sp_{r}") for r in ("tile", "unit", "summed", "limit"))
            count, load_ends, ends_left = end_counts(sp, "sp")

            def lone_wait(sem, value):
                sp.wait_ge(sem, value)
                sp.sem_inc(loads_passed, 1)

            def store_sums(u):
                with sp.While(lambda: ends_left(u) > 0):
                    i = sp.snap(tile, min_val=0, max_val=TILES - 1)
                    lone_wait(parked, i + 2)
                    lone_wait(in_dram, i * 16 + 32)
                    sp.dma_start(park[bass.ds((TILES - 1 - i) * P, P)],
                                 staged[:, bass.ds((i & 1) * D, D)]).then_inc(in_dram, 16)
                    sp.reg_add(tile, tile, 1)
                    sp.reg_sub(count[u], count[u], 1)

            half_of = lambda a: a.rearrange("(h p) d -> p h d", p=P)

            def load_sums(m, below):
                lone_wait(agg_added, 2 * m + 2)
                sp.dma_start(by_half(self_rows[:, :]), half_of(table[last_row_pair(below)])).then_inc(self_tile, 16)
                lone_wait(gnn_done, m + 1)
                sp.dma_start(by_half(agg), half_of(park[last_row_pair(below)])).then_inc(agg_ready, 16)

            def load_x1(m, below):
                lone_wait(base_ready, m + 1)
                sp.dma_start(by_half(x1[:, :]), half_of(x[last_row_pair(below)])).then_inc(x_tile, 16)

            def sums_ahead():
                with sp.If(sp.snap(summed) < sp.snap(unit) + 1):
                    m = sp.snap(summed, min_val=0, max_val=PAIRS - 1)
                    lone_wait(in_dram, m * 32 + 64)
                    load_sums(m, PAIRS - 1 - m)
                    sp.reg_add(summed, summed, 1)

            def next_unit():
                sums_ahead()
                m = sp.snap(unit, min_val=0, max_val=PAIRS - 1)
                load_x1(m, PAIRS - 1 - m)
                sp.reg_add(unit, unit, 1)

            def pairs_ready():
                return sp.snap(tile, min_val=0, max_val=TILES) >> 1

            sp.wait_ge(ready, 1)
            sp.reg_mov(tile, 0)
            sp.reg_mov(unit, 0)
            sp.reg_mov(summed, 0)
            with sp.Fori(0, ITERS) as it:
                load_ends(it)
                sp.reg_mov(limit, pairs_ready())
                with sp.If(sp.snap(unit) < sp.snap(limit)):
                    next_unit()
                for u in range(SLOTS):
                    sp.wait_ge(row_in[u], (it + 1) * (16 * CHUNKS))
                    sp.dma_start(idx[:, u * CHUNKS:(u + 1) * CHUNKS],
                                 src[(it + 1) * SLOTS + u]).then_inc(idx_in[u], 16)
                    store_sums(u)
                    if u == PREFETCH:
                        sp.reg_mov(limit, pairs_ready())
                        with sp.If(sp.snap(unit) < sp.snap(limit)):
                            sums_ahead()
            with sp.While(lambda: sp.snap(unit) < PAIRS):
                next_unit()
            load_sums(PAIRS, 0)
            load_x1(PAIRS, 0)
            for u in range(SLOTS):
                sp.wait_ge(idx_in[u], (ITERS + 1) * 16)

        @block.gpsimd
        def _(pool):
            pool.iota(node_row[:, :], [[1, P]], base=0, channel_multiplier=0,
                      allow_small_or_imprecise_dtypes=True).then_inc(iotas, 1)
            pool.iota(part_col[:, :], [[0, 1]], base=0, channel_multiplier=1,
                      allow_small_or_imprecise_dtypes=True).then_inc(iotas, 1)
            pool.iota(tile_base[:, 0:TILES + 1], [[-P, TILES + 1]], base=(TILES - 1) * P,
                      channel_multiplier=0, allow_small_or_imprecise_dtypes=True).then_inc(iotas, 1)
            pool.iota(tile_start[:, :], [[0, 1]], base=(TILES - 1) * P, channel_multiplier=-P,
                      allow_small_or_imprecise_dtypes=True).then_inc(iotas, 1)
            pool.iota(expert_row[:, :], [[1, EXPERTS]], base=0, channel_multiplier=0,
                      allow_small_or_imprecise_dtypes=True).then_inc(iotas, 1)

            def lone_wait(sem, value):
                pool.wait_ge(sem, value)
                pool.sem_inc(pool_passed, 1)

            def ln_scales(i, k):
                b = i * LN_BUFFERS + k
                c = k * LN_TILES
                moments = ln_mv[:, 2 * c:2 * c + 2 * LN_TILES]
                rstd_k, nmr_k = ln_rstd[:, c:c + LN_TILES], ln_nmr[:, c:c + LN_TILES]
                lone_wait(moments_ready, b + 1)
                if not first(i):
                    lone_wait(feat_ready, (b - LN_BUFFERS + 1) * LN_TILES)
                inverse_sqrt(pool, lone_wait, rstd_k, moments[:, 1::2], ln_half[:, :], ln_work[:, :],
                             ln_scale_step, b * (LN_SQRT_STEPS + 1), FSCALE)
                pool.tensor_scalar(ln_work[:, :], moments[:, 0::2], -1.0, None, ALU.mult).then_inc(ln_scale_step, 1)
                lone_wait(ln_scale_step, (b + 1) * (LN_SQRT_STEPS + 1))
                pool.tensor_tensor(nmr_k, ln_work[:, :], rstd_k, ALU.mult).then_inc(stats_ready, 1)

            over_batches(pool, ln_scales)
            wait_table(pool)

            def gather(it, u):
                lone_wait(idx_in[u], (it + 1) * 16)
                for j in range(CHUNKS):
                    c = u * CHUNKS + j
                    pool.indirect_dma_start(
                        rows[:, c * 2 * D:(c + 1) * 2 * D], None, table,
                        bass.IndirectOffsetOnAxis(ap=idx[:, c:c + 1], axis=0)).then_inc(row_in[u], 16)

            for u in range(SLOTS):
                gather(0, u)
            with pool.Fori(1, ITERS) as it:
                for u in range(SLOTS):
                    pool.wait_ge(slot_free[u], it)
                    gather(it, u)

        @block.vector
        def _(v):
            n = 0

            def own(ins):
                nonlocal n
                n += 1
                ins.then_inc(set_up, 1)

            own(v.memset(ends[:, :], 0))
            own(v.memset(ones_col[:, :], 1.0))
            own(v.memset(dst_f[:, GROUPS * CHUNKS:], float(FAR)))
            def lone_wait(sem, value):
                v.wait_ge(sem, value)
                v.sem_inc(vector_passed, 1)

            def moments(i, k):
                b = i * LN_BUFFERS + k
                if not (first(i) and k == 0):
                    v.wait_ge(moments_ready, b)
                v.wait_ge(x_in[k], i * 16 + 16)
                for t in range(LN_TILES):
                    ins = v.bn_stats(stats[:, 6 * t:6 * t + 6], ln_x[k][:, t * D:(t + 1) * D])
                ins.then_inc(ln_step, 1)
                if not first(i):
                    lone_wait(stats_ready, b - LN_BUFFERS + 1)
                lone_wait(ln_step, b + 1)
                at = 2 * k * LN_TILES
                for t in range(LN_TILES):
                    ins = v.bn_aggr(ln_mv[:, at + 2 * t:at + 2 * t + 2], stats[:, 6 * t:6 * t + 6])
                ins.then_inc(moments_ready, 1)

            def low(b, k):
                v.wait_ge(hi_ready, b + 1)
                hi_lo = ln_t[k].rearrange("p (t c) -> p t c", c=2 * D)
                v.tensor_tensor(hi_lo[:, :, D:2 * D], ln_f[k].rearrange("p (t d) -> p t d", d=D),
                                hi_lo[:, :, 0:D], ALU.subtract).then_inc(lo_ready, 1)

            def ln_batch(i, k):
                moments(i, k)
                if not (first(i) and k < 2):
                    low(i * LN_BUFFERS + k - 2, (k - 2) % LN_BUFFERS)

            over_batches(v, ln_batch)
            own(v.memset(comb[:, :], 0.0))
            own(v.memset(tok_hi[:, :].bitcast(F32), 0.0))
            own(v.memset(onehot[:, :], 0.0))
            own(v.memset(hid_hi[:, :].bitcast(F32), 0.0))
            v.memset(base[:, :], 0.0).then_inc(y_added, 1)
            v.memset(acc[:, :], 0.0).then_inc(y_added, 1)
            v.memset(hid_lo[:, :].bitcast(F32), 0.0).then_inc(hid_lo_ready, 1)
            v.memset(tok_lo[:, :].bitcast(F32), 0.0).then_inc(tok_lo_ready, 1)
            v.memset(lead[:, :], 0.0).then_inc(base_ready, 1)
            v.memset(mv[:, :], 0.0).then_inc(parked, 1)
            v.memset(comb_a[:, :], 0.0).then_inc(in_dram, 32)
            v.memset(comb_b[:, :], 0.0).then_inc(stored, 16)
            v.memset(scratch[:, :], 0.0).then_inc(agg_added, 2)
            for b in (LN_BATCHES - 2, LN_BATCHES - 1):
                low(b, b % LN_BUFFERS)

            v.wait_ge(iotas, 5)
            own(v.tensor_scalar(ident[:, :], node_row[:, :], part_col[:, 0:1], None, ALU.is_equal))
            own(v.tensor_scalar(ident16[:, :], node_row[:, :], part_col[:, 0:1], None, ALU.is_equal))
            v.wait_ge(consts, 16 * 6)
            own(v.tensor_copy(group_max_f, group_max_i))
            own(v.tensor_copy(dst_f[:, 0:GROUPS * CHUNKS], dst_i))
            parts = router[:, :].rearrange("p (k s e) -> p k s e", s=2, e=EXPERTS)
            raw = router_raw[:, :].rearrange("p (k e) -> p k e", e=EXPERTS)
            own(v.tensor_copy(parts[:, :, 0, :], raw))
            v.wait_ge(set_up, n)
            own(v.tensor_tensor(parts[:, :, 1, :], raw, parts[:, :, 0, :].bitcast(F32), ALU.subtract))
            own(v.tensor_scalar(reaches, group_max_f, tile_start[:, 0:1], None, ALU.is_ge))
            assert n == SETUP_STEPS
            v.wait_ge(counted, 1)
            own(v.tensor_copy(reached, ps_g[0:1, :]))
            v.wait_ge(set_up, n)
            own(v.tensor_tensor(ends[:, 0:MAXES - 1], reached[:, 0:MAXES - 1], reached[:, 1:MAXES], ALU.subtract))
            v.wait_ge(set_up, n)
            v.tensor_copy(scratch[:, :], ones_col[:, :]).then_inc(ready, 1)
            wait_table(v)

            step, used, tile, unit, limit = (v.alloc_register(f"v_{r}") for r in (
                "step", "used", "tile", "unit", "limit"))
            count, load_ends, ends_left = end_counts(v, "v")

            def one_hot(group, i):
                s = v.snap(step, min_val=0, max_val=GROUPS + TILES + 2)
                v.wait_ge(onehot_free, s + 1)
                at = (s & (RING - 1)) * (CHUNKS * P)
                v.scalar_tensor_tensor(
                    onehot[:, bass.ds(at, CHUNKS * P)].rearrange("p (c n) -> p c n", n=P),
                    node_row[:, :].unsqueeze(1).to_broadcast([P, CHUNKS, P]),
                    tile_base[:, bass.ds(i, 1)],
                    dst_f[:, bass.ds(group * CHUNKS, CHUNKS)].unsqueeze(2).to_broadcast([P, CHUNKS, P]),
                    ALU.add, ALU.is_equal).then_inc(onehot_ready, 1)
                v.reg_add(step, step, 1)

            def low_weights(u):
                raw, hi, lo = ((raw_w1, w1_hi, w1_lo), (raw_w2, w2_hi, w2_lo))[u // 4]
                at = slice(u % 4 * (WCOLS // 4), (u % 4 + 1) * (WCOLS // 4))
                v.wait_ge(w_hi, u // 4 + 1)
                v.tensor_tensor(lo[:, at], raw[:, at], hi[:, at].bitcast(F32), ALU.subtract).then_inc(w_lo, 1)

            def tile_value():
                return v.snap(tile, min_val=0, max_val=TILES)

            def prepare(group, u):
                one_hot(group, tile_value())
                with v.If(ends_left(u) > 0):
                    one_hot(group, v.snap(tile, min_val=0, max_val=TILES - 1) + 1)

            def walk(it, u):
                v.reg_add(used, used, 1)
                with v.While(lambda: ends_left(u) > 0):
                    v.wait_ge(onehot_free, v.snap(used, min_val=1, max_val=GROUPS + TILES + 2) + RING)
                    i = v.snap(tile, min_val=0, max_val=TILES - 1)
                    v.wait_ge(in_dram, i * 16 + 16)
                    at = (i & 1) * 512
                    v.tensor_reduce(staged[:, bass.ds((i & 1) * D, D)],
                                    sums[:, bass.ds(at, 2 * D)].rearrange("p (h d) -> p d h", h=2),
                                    mybir.AxisListType.X, ALU.add).then_inc(parked, 1)
                    v.reg_add(tile, tile, 1)
                    v.reg_add(used, used, 1)
                    v.reg_sub(count[u], count[u], 1)
                    with v.If(ends_left(u) > 0):
                        one_hot(it * SLOTS + u, v.snap(tile, min_val=0, max_val=TILES - 1) + 1)
                if u == SLOTS - 1:
                    load_ends(it + 1)
                prepare(it * SLOTS + u + 1, (u + 1) % SLOTS)

            def routed(ins, m, k, alone=False):
                ins.then_inc(route, 1)
                (lone_wait if alone else v.wait_ge)(route, m * ROUTE_STEPS + k)

            def read_logits(m):
                v.wait_ge(logits_done, m + 1)
                routed(v.tensor_reduce(logit[:, :].rearrange("p (h e) -> p h e", h=2),
                                       ps_t[:, 0:4 * EXPERTS].rearrange("p (h s e) -> p h e s", h=2, s=2),
                                       mybir.AxisListType.X, ALU.add), m, 1, alone=True)

            def top_experts(m):
                v.max(top[:, 0:8], logit[:, 0:EXPERTS])
                routed(v.max(top[:, 8:16], logit[:, EXPERTS:]), m, 2, alone=True)
                v.max_index(top_i[:, 0:8], top[:, 0:8], logit[:, 0:EXPERTS])
                routed(v.max_index(top_i[:, 8:16], top[:, 8:16], logit[:, EXPERTS:]), m, 3)
                by_tile = top[:, :].rearrange("p (h e) -> p h e", h=2)
                v.tensor_tensor(lead[:, :].unsqueeze(2), by_tile[:, :, 0:1], by_tile[:, :, 1:2],
                                ALU.subtract).then_inc(lead_ready, 1)
                routed(v.tensor_copy(top_f[:, :].rearrange("p (h e) -> p h e", h=2),
                                     top_i[:, :].rearrange("p (h e) -> p h e", h=2)[:, :, 0:2]), m, 4)

            def combine_weights(m):
                v.wait_ge(tanh_ready, m + 1)
                v.tensor_scalar(wgt[:, 0:4:2], tanh[:, :], 0.5, 0.5, ALU.mult, ALU.add)
                routed(v.tensor_scalar(wgt[:, 1:4:2], tanh[:, :], -0.5, 0.5, ALU.mult, ALU.add), m, 5)
                for h in (0, 1):
                    for k, part_of in enumerate((comb_a, comb_b)):
                        c = 2 * h + k
                        ins = v.tensor_scalar(part_of[:, h * EXPERTS:(h + 1) * EXPERTS], expert_row[:, :],
                                              top_f[:, c:c + 1], wgt[:, c:c + 1], ALU.is_equal, ALU.mult)
                routed(ins, m, 6)
                routed(v.tensor_tensor(comb[:, :], comb_a[:, :], comb_b[:, :], ALU.add), m, 7)

            def hid_low(m, e):
                at = slice((e & 1) * D2, (e & 1) * D2 + D2)
                v.wait_ge(hid_hi_ready, m * EXPERTS + e + 1)
                v.tensor_tensor(hid_lo[:, at], gel[:, at], hid_hi[:, at].bitcast(F32),
                                ALU.subtract).then_inc(hid_lo_ready, 1)

            def add_output(m, u):
                e = (u - 2) % EXPERTS
                v.wait_ge(y_done, m * EXPERTS + u + 1)
                v.wait_ge(y_added, m * EXPERTS + u + 2)
                if u == 6:
                    v.wait_ge(bias_added, m + 1)
                if e == EXPERTS - 1:
                    v.wait_ge(stored, m * 16 + 16)
                so_far = base if e == 0 else acc
                into = acc_out if e == EXPERTS - 1 else acc
                for h in (0, 1):
                    at = slice(h * D, (h + 1) * D)
                    ins = v.scalar_tensor_tensor(into[:, at], ps_y[e & 1][:, at],
                                                 comb[:, h * EXPERTS + e:h * EXPERTS + e + 1], so_far[:, at],
                                                 ALU.mult, ALU.add)
                ins.then_inc(y_added, 1)

            def add_bias(m):
                v.wait_ge(bias_done, m + 1)
                v.wait_ge(y_added, m * EXPERTS + 8)
                v.tensor_tensor(acc[:, :], acc[:, :], ps_g[:, :], ALU.add).then_inc(bias_added, 1)

            def add_self(m):
                v.wait_ge(agg_ready, m * 16 + 16)
                v.wait_ge(self_tile, m * 16 + 16)
                own_rows = self_rows[:, :].rearrange("p (h s d) -> p h s d", h=2, s=2)
                for s in (0, 1):
                    v.tensor_tensor(by_half(agg), by_half(agg), own_rows[:, :, s, :], ALU.add).then_inc(agg_added, 1)
                    if s == 0:
                        v.wait_ge(agg_added, 2 * m + 3)

            def residual(m):
                v.wait_ge(gnn_done, m + 2)
                v.wait_ge(x_tile, m * 16 + 16)
                v.scalar_tensor_tensor(x1[:, :], ps_g[:, :], 0.0, x1[:, :],
                                       ALU.max, ALU.add).then_inc(front, 1)
                v.wait_ge(front, m * FRONT_STEPS + 1)
                for h in (0, 1):
                    ins = v.bn_stats(stats[:, 6 * h:6 * h + 6], x1[:, h * D:(h + 1) * D])
                ins.then_inc(front, 1)
                lone_wait(front, m * FRONT_STEPS + 2)
                for h in (0, 1):
                    ins = v.bn_aggr(mv[:, 2 * h:2 * h + 2], stats[:, 6 * h:6 * h + 6])
                ins.then_inc(front, 1)

            def scale(m, steps):
                v.wait_ge(front, m * FRONT_STEPS + 3 + steps.start)
                inverse_sqrt(v, v.wait_ge, rstd[:, :], mv[:, 1:4:2], half[:, :], work[:, :],
                             front, m * FRONT_STEPS + 3, steps=steps)

            def normalize(m):
                for h in (0, 1):
                    at = slice(h * D, (h + 1) * D)
                    ins = v.tensor_scalar(normed[:, at], x1[:, at], mv[:, 2 * h:2 * h + 1], rstd[:, h:h + 1],
                                          ALU.subtract, ALU.mult)
                ins.then_inc(normed_ready, 1)

            def part(m, u):
                if u == 0:
                    add_self(m)
                if u == 1:
                    read_logits(m)
                if u == 2:
                    combine_weights(m)
                if u == 4:
                    v.wait_ge(comb_td, m + 1)
                    v.tensor_copy(comb_t[:, :], ps_t[0:EXPERTS, 0:P2]).then_inc(comb_tr, 1)
                if u == 6:
                    scale(m, range(9, SQRT_STEPS))
                    normalize(m)
                add_output(m, u)
                if u == 1:
                    top_experts(m)
                if u == 3:
                    residual(m)
                if u == 4:
                    scale(m, range(0, 5))
                if u == 5:
                    scale(m, range(5, 9))
                if u == EXPERTS - 1:
                    v.wait_ge(tok_hi_ready, m + 1)
                    v.tensor_tensor(tok_lo[:, :], ps_t[:, :], tok_hi[:, :].bitcast(F32),
                                    ALU.subtract).then_inc(tok_lo_ready, 1)
                hid_low(m, u)
                if u == EXPERTS - 1:
                    v.wait_ge(normed_ready, m + 1)
                    v.tensor_tensor(base[:, :], x1[:, :], normed, ALU.add).then_inc(base_ready, 1)
                if u == 5:
                    add_bias(m)

            def unit_value():
                return v.snap(unit, min_val=0, max_val=UNITS - 1)

            v.reg_mov(step, 0)
            v.reg_mov(tile, 0)
            v.reg_mov(unit, 0)
            v.reg_mov(used, 0)
            load_ends(0)
            prepare(0, 0)
            for u in range(SLOTS):
                walk(0, u)
                low_weights(u)
            with v.Fori(1, ITERS) as it:
                v.reg_mov(limit, tile_value() >> 1)
                with v.If(v.snap(unit) < v.snap(limit)):
                    m = unit_value()
                    for u in range(SLOTS):
                        walk(it, u)
                        part(m, u)
                    v.reg_add(unit, unit, 1)
                with v.Else():
                    for u in range(SLOTS):
                        walk(it, u)
            with v.While(lambda: v.snap(unit) < UNITS):
                for u in range(EXPERTS):
                    part(unit_value(), u)
                v.reg_add(unit, unit, 1)
            for u in (0, 1):
                add_output(UNITS, u)

        @block.tensor
        def _(pe):
            pe.wait_ge(set_up, SETUP_STEPS)
            pe.matmul(ps_g[0:1, :], ones_col[0:TILES, :], reaches[0:TILES, :], start=True, stop=True).then_inc(counted, 1)
            pe.wait_ge(ready, 1)
            for done in (agg_sum, gnn_done):
                pe.matmul(ps_t[:, 0:P], onehot[:, 0:P], onehot[:, 0:P], start=True, stop=True).then_inc(done, 1)
            for k in (0, 1):
                mm = pe.matmul(ps_y[k][:, :], onehot[:, 0:P], onehot[:, 0:512], start=True, stop=True)
            mm.then_inc(y_done, 1)
            for k in (0, 1):
                mm = pe.matmul(sums[:, 512 * k:512 * k + 512], onehot[:, 0:P], onehot[:, 0:512],
                               start=True, stop=True)
            mm.then_inc(onehot_free, RING)

            step1, tile1, at, bank, unit, limit = (pe.alloc_register(f"pe_{r}") for r in (
                "step1", "tile1", "at", "bank", "unit", "limit"))
            count, load_ends, ends_left = end_counts(pe, "pe")
            AT = RING * CHUNKS * P

            def sum_group(u, first, last_slot=None):
                a = pe.snap(at, min_val=0, max_val=AT - CHUNKS * P)
                b = pe.snap(bank, min_val=0, max_val=512)
                pe.wait_ge(onehot_ready, pe.snap(step1, min_val=1, max_val=GROUPS + TILES + 3))
                for j in range(CHUNKS):
                    c = u * CHUNKS + j
                    mm = pe.matmul(sums[:, bass.ds(b, 2 * D)], onehot[:, bass.ds(a + j * P, P)],
                                   rows[:, c * 2 * D:(c + 1) * 2 * D], start=(first and j == 0),
                                   stop=False, skip_group_check=True)
                    if j == 0 and last_slot is not None:
                        mm.then_inc(slot_free[last_slot], 1)
                mm.then_inc(onehot_free, 1)
                pe.reg_add(step1, step1, 1)
                pe.reg_add(at, at, CHUNKS * P)
                pe.reg_alu(at, at, AT - 1, ALU.bitwise_and)

            def walk(it, u, first_round=False):
                pe.wait_ge(row_in[u], (it + 1) * (16 * CHUNKS))
                sum_group(u, False, None if first_round and u == 0 else (u - 1) % SLOTS)
                with pe.While(lambda: ends_left(u) > 0):
                    pe.reg_alu(bank, bank, 512, ALU.bitwise_xor)
                    pe.wait_ge(parked, pe.snap(tile1, min_val=1, max_val=TILES + 1))
                    sum_group(u, True)
                    pe.reg_add(tile1, tile1, 1)
                    pe.reg_sub(count[u], count[u], 1)

            def hidden(m, e):
                if e == 0:
                    pe.wait_ge(tok_lo_ready, m + 1)
                for f in range(HALVES):
                    n = 0
                    for w, t in ((w1_hi, tok_hi), (w1_hi, tok_lo), (w1_lo, tok_hi)):
                        for k in range(HALVES):
                            mm = pe.matmul(ps_h[e & 1][:, f * P2:(f + 1) * P2],
                                           w[:, wcol(e, k, f):wcol(e, k, f) + P], t[:, k * P2:(k + 1) * P2],
                                           start=(n == 0), stop=(n == 3 * HALVES - 1))
                            n += 1
                mm.then_inc(h_done, 1)

            def output(m, u):
                e = (u - 1) % EXPERTS
                pe.wait_ge(hid_lo_ready, m * EXPERTS + u + 1)
                pe.wait_ge(y_added, m * EXPERTS + u + 2)
                for h in (0, 1):
                    n = 0
                    for t, w in ((hid_hi, w2_hi), (hid_hi, w2_lo), (hid_lo, w2_hi)):
                        for k in range(HALVES):
                            at = (e & 1) * D2 + k * P2 + h * P
                            mm = pe.matmul(ps_y[e & 1][:, h * D:(h + 1) * D], t[:, at:at + P],
                                           w[:, wcol(e, k):wcol(e, k) + D],
                                           start=(n == 0), stop=(n == 3 * HALVES - 1))
                            n += 1
                mm.then_inc(y_done, 1)

            def transpose_agg(m):
                pe.wait_ge(route, m * ROUTE_STEPS + 1)
                pe.wait_ge(agg_added, 2 * m + 4)
                for k in range(HALVES):
                    for h in (0, 1):
                        mm = pe.transpose(ps_t[:, k * P2 + h * P:k * P2 + (h + 1) * P],
                                          agg[:, h * D + k * P:h * D + (k + 1) * P], ident[:, :])
                mm.then_inc(agg_sum, 1)

            def graph_product(m):
                pe.wait_ge(agg_t, m + 1)
                for h in (0, 1):
                    for k in range(HALVES):
                        at = k * P2 + h * P
                        mm = pe.matmul(ps_g[:, h * D:(h + 1) * D], agg[:, at:at + P], gw_sb[:, k * D:(k + 1) * D],
                                       start=(k == 0), stop=(k == HALVES - 1))
                mm.then_inc(gnn_done, 1)

            def logits(m):
                for h in (0, 1):
                    for t, cols in ((tok_hi, 2 * EXPERTS), (tok_lo, EXPERTS)):
                        for k in range(HALVES):
                            at = k * P2 + h * P
                            mm = pe.matmul(ps_t[:, 2 * h * EXPERTS:2 * h * EXPERTS + cols], t[:, at:at + P],
                                           router[:, 2 * k * EXPERTS:2 * k * EXPERTS + cols],
                                           start=(t is tok_hi and k == 0), stop=(t is tok_lo and k == HALVES - 1),
                                           skip_group_check=True)
                mm.then_inc(logits_done, 1)

            def part(m, u):
                if u == EXPERTS - 1:
                    pe.wait_ge(normed_ready, m + 1)
                    for k in range(HALVES):
                        for h in (0, 1):
                            mm = pe.transpose(ps_t[:, k * P2 + h * P:k * P2 + (h + 1) * P],
                                              normed[:, h * D + k * P:h * D + (k + 1) * P], ident[:, :])
                    mm.then_inc(tok_t, 1)
                hidden(m, u)
                output(m, u)
                if u == 0:
                    logits(m)
                if u == 1:
                    transpose_agg(m)
                if u == 2:
                    graph_product(m)
                if u == 3:
                    pe.wait_ge(route, (m + 1) * ROUTE_STEPS)
                    for h in (0, 1):
                        mm = pe.transpose(ps_t[0:EXPERTS, h * P:(h + 1) * P],
                                          comb[:, h * EXPERTS:(h + 1) * EXPERTS], ident[:, :])
                    mm.then_inc(comb_td, 1)
                if u == 4:
                    pe.wait_ge(front, m * FRONT_STEPS + 1)
                    pe.wait_ge(comb_tr, m + 1)
                    for h in (0, 1):
                        mm = pe.matmul(ps_g[:, h * D:(h + 1) * D], comb_t[:, h * P:(h + 1) * P], b2_sb[:, :],
                                       start=True, stop=True)
                    mm.then_inc(bias_done, 1)

            def unit_value():
                return pe.snap(unit, min_val=0, max_val=UNITS - 1)

            for register, value in ((step1, 1), (tile1, 1), (at, 0), (bank, 0), (unit, 0)):
                pe.reg_mov(register, value)
            load_ends(0)
            for u in range(SLOTS):
                walk(0, u, first_round=True)
            load_ends(1)
            pe.wait_ge(w_lo, 8)
            with pe.Fori(1, ITERS) as it:
                pe.reg_mov(limit, (pe.snap(tile1, min_val=1, max_val=TILES + 1) - 1) >> 1)
                with pe.If(pe.snap(unit) < pe.snap(limit)):
                    m = unit_value()
                    for u in range(SLOTS):
                        walk(it, u)
                        part(m, u)
                    pe.reg_add(unit, unit, 1)
                with pe.Else():
                    for u in range(SLOTS):
                        walk(it, u)
                load_ends(it + 1)
            with pe.While(lambda: pe.snap(unit) < UNITS):
                for u in range(EXPERTS):
                    part(unit_value(), u)
                pe.reg_add(unit, unit, 1)
            output(UNITS, 0)

        @block.scalar
        def _(act):
            tb = table.rearrange("(b t p) c -> b p t c", p=P, t=LN_TILES)

            def features(i, k):
                b = i * LN_BUFFERS + k
                act.wait_ge(stats_ready, b + 1)
                if not first(i):
                    act.wait_ge(lo_ready, b - LN_BUFFERS + 1)
                for t in range(LN_TILES):
                    c = k * LN_TILES + t
                    act.activation(ln_f[k][:, t * D:(t + 1) * D], ln_x[k][:, t * D:(t + 1) * D], ACT.Identity,
                                   bias=ln_nmr[:, c:c + 1], scale=ln_rstd[:, c:c + 1]).then_inc(feat_ready, 1)

            def store(b, k):
                act.wait_ge(lo_ready, b + 1)
                act.dma_start(tb[b], ln_t[k].rearrange("p (t c) -> p t c", c=2 * D)).then_inc(t_out[k], 16)

            def ln_batch(i, k):
                b = i * LN_BUFFERS + k
                features(i, k)
                if not (first(i) and k == 0):
                    store(b - 1, (k - 1) % LN_BUFFERS)
                if not first(i):
                    act.wait_ge(t_out[k], i * 16)
                act.wait_ge(feat_ready, (b + 1) * LN_TILES)
                act.activation(ln_t[k].rearrange("p (t c) -> p t c", c=2 * D)[:, :, 0:D],
                               ln_f[k].rearrange("p (t d) -> p t d", d=D), ACT.Copy).then_inc(hi_ready, 1)

            act.wait_ge(set_up, 2)
            act.activation(scratch_act[:, :], ones_col[:, :], ACT.Gelu)
            over_batches(act, ln_batch)
            store(LN_BATCHES - 1, (LN_BATCHES - 1) % LN_BUFFERS)
            for k, (raw, hi) in enumerate(((raw_w1, w1_hi), (raw_w2, w2_hi))):
                act.wait_ge(weights_in, 32)
                act.activation(hi[:, :], raw, ACT.Copy).then_inc(w_hi, 1)
            wait_table(act)
            act.wait_ge(ready, 1)

            def unit(m):
                for e in range(EXPERTS):
                    act.wait_ge(h_done, m * EXPERTS + e + 1)
                    at = (e & 1) * D2
                    if e == EXPERTS - 1:
                        act.wait_ge(tok_t, m + 1)
                        act.activation(tok_hi[:, :], ps_t[:, :], ACT.Copy).then_inc(tok_hi_ready, 1)
                    for f in range(HALVES):
                        g = act.activation(gel[:, at + f * P2:at + (f + 1) * P2],
                                           ps_h[e & 1][:, f * P2:(f + 1) * P2], ACT.Gelu,
                                           bias=b1_sb[:, e * HALVES + f:e * HALVES + f + 1])
                    g.then_inc(gel_ready, 1)
                    act.wait_ge(gel_ready, m * EXPERTS + e + 1)
                    act.activation(hid_hi[:, at:at + D2], gel[:, at:at + D2], ACT.Copy).then_inc(hid_hi_ready, 1)
                    if e == 1:
                        act.wait_ge(lead_ready, m + 1)
                        act.activation(tanh[:, :], lead[:, :], ACT.Tanh, scale=0.5).then_inc(tanh_ready, 1)
                        act.wait_ge(agg_sum, m + 2)
                        act.activation(agg, ps_t[:, :], ACT.Copy, scale=1.0 / FSCALE).then_inc(agg_t, 1)
                    if e == 2:
                        store_result(m)

            def store_result(m):
                act.wait_ge(y_added, m * EXPERTS + 4)
                act.dma_start(out[last_row_pair(UNITS - m)].rearrange("(h p) d -> p h d", p=P),
                              by_half(acc_out[:, :])).then_inc(stored, 16)

            with act.Fori(0, UNITS) as m:
                unit(m)
            store_result(UNITS)
            act.wait_ge(stored, (UNITS + 2) * 16)


def kernel(**inputs):
    import numpy as np
    from concourse import bacc
    from concourse.bass_utils import run_bass_kernel_spmd

    a = {k: np.asarray(v) for k, v in inputs.items()}
    padded = GROUPS * GROUP
    src = np.zeros(padded, np.int32)
    dst = np.full(padded, FAR, np.int32)
    src[padded - EDGES:] = a["src"][::-1]
    dst[padded - EDGES:] = a["dst"][::-1]
    group_max = np.full((P, MAXES), -1, np.int32)
    group_max[:, :GROUPS] = dst[::GROUP]
    x = np.zeros((ROWS, D), np.float32)
    x[:NODES] = a["x"]
    arrays = {
        "x": x,
        "src": np.ascontiguousarray(np.concatenate([src, np.zeros(SLOTS * GROUP, np.int32)]).reshape(GROUPS + SLOTS, P, CHUNKS)),
        "dst": np.ascontiguousarray(dst.reshape(GROUPS, P, CHUNKS).transpose(1, 0, 2).reshape(P, GROUPS * CHUNKS)),
        "group_max": group_max,
        "gw": a["L0_gnn_weight1"],
        "router": np.ascontiguousarray(a["L0_ffn_router_w"].T),
        "w1": a["L0_ffn_w1"],
        "b1": np.ascontiguousarray(a["L0_ffn_b1"].reshape(EXPERTS, HALVES, P).transpose(2, 0, 1).reshape(P, EXPERTS * HALVES)),
        "w2": a["L0_ffn_w2"],
        "b2": a["L0_ffn_b2"],
    }
    nc = bacc.Bacc("TRN2", target_bir_lowering=False, num_devices=1)
    args = [nc.dram_tensor(f"in_{n}", v.shape, mybir.dt.from_np(v.dtype), kind="ExternalInput").ap()
            for n, v in arrays.items()]
    out = nc.dram_tensor("out_0", (ROWS + 2 * P2, D), F32, kind="ExternalOutput").ap()
    build(nc, *args, out)
    r = run_bass_kernel_spmd(nc, [{f"in_{n}": v for n, v in arrays.items()}], core_ids=[0])
    return r.results[0]["out_0"][:NODES]
```
